# Optimizing a Trainium2 kernel written in Bass

```python
import numpy as np
import jax
import jax.numpy as jnp

def _softmax(x, axis=-1):
    return jax.nn.softmax(x, axis=axis)

def _gelu(x):
    return jax.nn.gelu(x, approximate=True)

def _silu(x):
    return jax.nn.silu(x)

def _sigmoid(x):
    return jax.nn.sigmoid(x)

def _layernorm(x, axis=-1, eps=1e-05):
    m = jnp.mean(x, axis=axis, keepdims=True)
    v = jnp.var(x, axis=axis, keepdims=True)
    return (x - m) / jnp.sqrt(v + eps)

def _scatter_add(tgt, idx, src, axis=0):
    return tgt.at[idx].add(src)

def _segment_sum(src, seg, n):
    return jax.ops.segment_sum(src, seg, n)
kernel_name = 'mk_xattn_ffn_d1_seqx_r8_d59c8d'

def setup_inputs(seed: int=0):
    np.random.seed(seed)
    _w = jnp.asarray

    def _rec_inputs():
        import jax
        import jax.numpy as jnp
        _rk = jax.random.key(seed)
        x = 7.22e-05 + 1 * jax.random.normal(jax.random.fold_in(_rk, 1), (64, 64, 256), jnp.float32)
        _lenS = 64 - jax.random.randint(jax.random.fold_in(_rk, 7), (64,), 0, max(1, 64 // 4) + 1, jnp.int32)
        _lenS2 = 64 - jax.random.randint(jax.random.fold_in(_rk, 8), (64,), 0, max(1, 64 // 4) + 1, jnp.int32)
        _ctx_1024P = jax.random.normal(jax.random.fold_in(_rk, 11), (64, 16, 128), jnp.float32)
        _ctx_1024c = jax.random.dirichlet(jax.random.fold_in(_rk, 511), 0.3 * jnp.ones((16,), jnp.float32), (64, 64))
        _ctx_1024t = jnp.einsum('bsk,bkd->bsd', _ctx_1024c, _ctx_1024P)
        _ctx_1024t = _ctx_1024t * jax.lax.rsqrt(jnp.mean(jnp.square(_ctx_1024t)) + 1e-12) * 0.953939
        ctx_1024 = -1.39393e-06 + 0.999914 * (_ctx_1024t + 0.3 * jax.random.normal(jax.random.fold_in(_rk, 611), (64, 64, 128), jnp.float32))
        fside_BxSx2_0 = jax.random.uniform(jax.random.fold_in(_rk, 12), (64, 64, 2), jnp.float32, 0.0, 0.999707)
        return (x, ctx_1024, fside_BxSx2_0)
    x, ctx_1024, fside_BxSx2_0 = _rec_inputs()

    def _L0_xattn_setup():
        import jax, jax.numpy as jnp
        import numpy as np
        DIM = 256
        CTX_DIM = 128
        N_HEADS = 32
        HEAD_DIM = DIM // N_HEADS
        POS_DIM = 2
        B, N, CTXN = (2, 256, 256)
        ROPE_BASE = 10000.0

        def apply_axial_rope(x, pos):
            b, n, h, d = x.shape
            p = pos.shape[-1]
            dpa = d // p
            half = dpa // 2
            freqs = ROPE_BASE ** (-jnp.arange(half, dtype=x.dtype) / half)
            ang = pos[..., :, None] * freqs
            cos = jnp.cos(ang)[:, :, None, :, :]
            sin = jnp.sin(ang)[:, :, None, :, :]
            xr = x.reshape(b, n, h, p, half, 2)
            x1, x2 = (xr[..., 0], xr[..., 1])
            out = jnp.stack([x1 * cos - x2 * sin, x1 * sin + x2 * cos], axis=-1)
            return out.reshape(b, n, h, d)
        key = jax.random.key(seed)
        ks = jax.random.split(key, 8)
        x = jax.random.normal(ks[0], (B, N, DIM), jnp.float32)
        ctx = jax.random.normal(ks[1], (B, CTXN, CTX_DIM), jnp.float32)
        pos_map = jax.random.uniform(ks[2], (B, N, POS_DIM), jnp.float32)
        ctx_pos_map = jax.random.uniform(ks[3], (B, CTXN, POS_DIM), jnp.float32)
        Wq = jax.random.normal(ks[4], (DIM, DIM), jnp.float32) / np.sqrt(DIM)
        Wkv = jax.random.normal(ks[5], (CTX_DIM, 2 * DIM), jnp.float32) / np.sqrt(CTX_DIM)
        Wout = jax.random.normal(ks[6], (DIM, DIM), jnp.float32) / np.sqrt(DIM)
        bout = jnp.zeros((DIM,), jnp.float32)
        return {'x': x, 'ctx': ctx, 'pos_map': pos_map, 'ctx_pos_map': ctx_pos_map, 'Wq': Wq, 'Wkv': Wkv, 'Wout': Wout, 'bout': bout}
    _L0_xattn_all = _L0_xattn_setup()
    _L0_xattn_in = {k: v for k, v in _L0_xattn_all.items() if k in ('Wq', 'Wkv', 'Wout', 'bout')}
    del _L0_xattn_all

    def _L0_ffn_setup():
        import jax, jax.numpy as jnp
        import numpy as np
        TOP_K = 2
        key = jax.random.key(seed)
        ks = jax.random.split(key, 5)
        B, T, D, E, H = (4, 256, 256, 8, 176)
        s = 1.0 / np.sqrt(D)
        sh = 1.0 / np.sqrt(H)
        return {'x': jax.random.normal(ks[0], (B, T, D), dtype=jnp.float32), 'Wg': jax.random.normal(ks[1], (E, D), dtype=jnp.float32) * s, 'W1': jax.random.normal(ks[2], (E, H, D), dtype=jnp.float32) * s, 'W2': jax.random.normal(ks[3], (E, H, D), dtype=jnp.float32) * s, 'W3': jax.random.normal(ks[4], (E, D, H), dtype=jnp.float32) * sh}
    _L0_ffn_all = _L0_ffn_setup()
    _L0_ffn_in = {k: v for k, v in _L0_ffn_all.items() if k in ('Wg', 'W1', 'W2', 'W3')}
    del _L0_ffn_all
    return {'x': x, 'ctx_1024': ctx_1024, 'fside_BxSx2_0': fside_BxSx2_0, 'L0_xattn_Wq': _L0_xattn_in['Wq'], 'L0_xattn_Wkv': _L0_xattn_in['Wkv'], 'L0_xattn_Wout': _L0_xattn_in['Wout'], 'L0_xattn_bout': _L0_xattn_in['bout'], 'L0_ffn_Wg': _L0_ffn_in['Wg'], 'L0_ffn_W1': _L0_ffn_in['W1'], 'L0_ffn_W2': _L0_ffn_in['W2'], 'L0_ffn_W3': _L0_ffn_in['W3']}

def reference(x, ctx_1024, fside_BxSx2_0, L0_xattn_Wq, L0_xattn_Wkv, L0_xattn_Wout, L0_xattn_bout, L0_ffn_Wg, L0_ffn_W1, L0_ffn_W2, L0_ffn_W3):
    import jax
    import jax.numpy as jnp

    def _L0_xattn_ref(x, ctx, pos_map, ctx_pos_map, Wq, Wkv, Wout, bout):
        import jax, jax.numpy as jnp
        import numpy as np
        DIM = 256
        CTX_DIM = 128
        N_HEADS = 32
        HEAD_DIM = DIM // N_HEADS
        POS_DIM = 2
        B, N, CTXN = (2, 256, 256)
        ROPE_BASE = 10000.0

        def apply_axial_rope(x, pos):
            b, n, h, d = x.shape
            p = pos.shape[-1]
            dpa = d // p
            half = dpa // 2
            freqs = ROPE_BASE ** (-jnp.arange(half, dtype=x.dtype) / half)
            ang = pos[..., :, None] * freqs
            cos = jnp.cos(ang)[:, :, None, :, :]
            sin = jnp.sin(ang)[:, :, None, :, :]
            xr = x.reshape(b, n, h, p, half, 2)
            x1, x2 = (xr[..., 0], xr[..., 1])
            out = jnp.stack([x1 * cos - x2 * sin, x1 * sin + x2 * cos], axis=-1)
            return out.reshape(b, n, h, d)
        b, n, _ = x.shape
        ctx_n = ctx.shape[1]
        q = (x @ Wq).reshape(b, n, N_HEADS, HEAD_DIM)
        k, v = jnp.split(ctx @ Wkv, 2, axis=-1)
        k = k.reshape(b, ctx_n, N_HEADS, HEAD_DIM)
        v = v.reshape(b, ctx_n, N_HEADS, HEAD_DIM)
        q = apply_axial_rope(q, pos_map)
        k = apply_axial_rope(k, ctx_pos_map)
        scale = 1.0 / np.sqrt(HEAD_DIM).astype(np.float32)
        logits = jnp.einsum('bqhd,bkhd->bhqk', q, k) * scale
        w = jax.nn.softmax(logits, axis=-1)
        attn = jnp.einsum('bhqk,bkhd->bqhd', w, v)
        attn = attn.reshape(b, n, N_HEADS * HEAD_DIM)
        return attn @ Wout + bout

    def _L0_ffn_ref(x, Wg, W1, W2, W3):
        import jax, jax.numpy as jnp
        import numpy as np
        TOP_K = 2
        E = Wg.shape[0]
        scores = jnp.einsum('btd,ed->bte', x, Wg)
        topk_s, topk_i = jax.lax.top_k(scores, TOP_K)
        probs = jax.nn.softmax(topk_s, axis=-1)
        onehot = (topk_i[..., None] == jnp.arange(E)).astype(x.dtype)
        w = jnp.einsum('btk,btke->bte', probs, onehot)
        y = jnp.zeros_like(x)
        for e in range(E):
            h = jax.nn.silu(jnp.einsum('btd,hd->bth', x, W1[e])) * jnp.einsum('btd,hd->bth', x, W2[e])
            y = y + w[..., e:e + 1] * jnp.einsum('bth,dh->btd', h, W3[e])
        return y
    x = x + _L0_xattn_ref(_layernorm(x, axis=-1), ctx_1024, fside_BxSx2_0, fside_BxSx2_0, L0_xattn_Wq, L0_xattn_Wkv, L0_xattn_Wout, L0_xattn_bout)
    x = x + _L0_ffn_ref(_layernorm(x, axis=-1), L0_ffn_Wg, L0_ffn_W1, L0_ffn_W2, L0_ffn_W3)
    return x

_drawn_inputs = setup_inputs


def setup_inputs(seed=0):
    import zlib

    import numpy as np

    out = dict(_drawn_inputs(seed))
    spreads = {'L0_xattn_bout': (0.0, 0.1)}
    factors = {}
    for name, (base, spread) in spreads.items():
        noise = np.random.default_rng([zlib.crc32(name.encode()), seed]).standard_normal(out[name].shape)
        drawn = base * np.exp(spread * noise) if base else spread * noise
        out[name] = jnp.asarray(drawn.astype(out[name].dtype))
    for name, factor in factors.items():
        out[name] = (out[name] * factor).astype(out[name].dtype)
    return out
```

```python
import math
from contextlib import ExitStack

import numpy as np

import concourse.bass as bass
from concourse import mybir

P = 128
ALU = mybir.AluOpType
ACT = mybir.ActivationFunctionType
F32 = mybir.dt.float32
BF16 = mybir.dt.bfloat16
I32 = mybir.dt.int32
U32 = mybir.dt.uint32
AX_X = mybir.AxisListType.X
MAGIC = 1.5 * 2.0 ** 23
EPS = 1e-5


class Tile:

    def __init__(self, i, c):
        self.i, self.c = i, c

    def plus(self, d):
        return Tile(self.i, self.c + d)

    @property
    def n(self):
        return self.i * 2 + self.c

    @property
    def half(self):
        return self.i + self.c // 2

    @property
    def par(self):
        return self.c % 2

    def times(self, m, d=0):
        return self.i * (2 * m) + (self.c * m + d)


def xattn_ffn_kernel(nc, x, ctx_in, pos, Wq, Wkv, Wout, bout, Wg, W1, W2, W3, out):
    B, N, D = x.shape
    CD = ctx_in.shape[2]
    E, H, _ = W1.shape
    TOKENS = B * N
    T = TOKENS // P
    KC = D // P
    HEADS, HD = 32, 8
    GH = 8
    G = HEADS // GH
    GW = GH * HD
    SCALE = float(np.float32(1.0) / np.sqrt(np.float32(HD)))
    HA = 96
    HB = H - HA
    OVER = HA - HB
    RC = TOKENS + P
    NBLK = 2 * TOKENS // P + E - 1
    SPARE = E - 1
    RW = D + 1
    NOWHERE = 1 << 20
    assert N == 64 and P == 2 * N and T % 2 == 0 and NBLK % 2 == 1 and CD == P and D == 2 * P

    x_rows = x.rearrange("b n d -> (b n) d")
    ctx_rows = ctx_in.rearrange("b n d -> (b n) d")
    out_rows = out.rearrange("b n d -> (b n) d")
    pos_rows = pos.rearrange("b n c -> (b n) c").rearrange("(t p) c -> p t c", p=P)
    routed = nc.dram_tensor("routed_rows", (E * RC + SPARE * P, RW), F32, kind="Internal").ap()
    results = nc.dram_tensor("result_rows", (2 * TOKENS, D), F32, kind="Internal").ap()

    with ExitStack() as es:
        def sb(name, shape, dt=F32):
            return es.enter_context(nc.sbuf_tensor(name, shape, dt))

        def sem(name):
            return es.enter_context(nc.semaphore(name))

        banks = [es.enter_context(nc.psum_tensor(f"bank{n}", [P, 512], F32)) for n in range(8)]
        ps_l, ps_pt, ps_qk, ps_vo, ps_nd, ps_tr = banks[0:2], banks[2:4], banks[4], banks[5], banks[6], banks[7]

        xres = sb("xres", [P, T, D])
        ctx_sb = sb("ctx_sb", [P, 2, CD])
        xn = sb("xn", [P, 2, D])
        stats = sb("stats", [P, 2, 6])
        mv1 = sb("mv1", [P, 2, 2])
        rstd1 = sb("rstd1", [P, 2])
        mv2 = sb("mv2", [P, 2, 2])
        rstd2 = sb("rstd2", [P, 2])
        var_eps1 = sb("var_eps1", [P, 1])
        var_eps2 = sb("var_eps2", [P, 1])
        minus_half = sb("minus_half", [P, 1])
        xT = sb("xT", [P, 3 * P])
        rope_a = sb("rope_a", [P, 512])
        rope_b = sb("rope_b", [P, 512])
        rot = sb("rot", [P, 512])
        kT = sb("kT", [P, 2, G, N])
        qbd = sb("qbd", [P, 2, G, P])
        km = sb("km", [P, 2, G, GH, N])
        vst = sb("vst", [P, 2, 2 * HEADS // 2, 32])
        rowmax = sb("rowmax", [P, 2, GH])
        shifted = sb("shifted", [P, 2, 512])
        expd = sb("expd", [P, 2, 512])
        pT = sb("pT", [P, G, 512])
        rden = sb("rden", [P, D])
        attnT = sb("attnT", [P, D])
        xs = sb("xs", [P, 2, 2, RW])
        x2T = sb("x2T", [P, D])
        top8 = sb("top8", [P, 8])
        idx8 = sb("idx8", [P, 8], U32)
        idxf = sb("idxf", [P, 2])
        onehot = sb("onehot", [P, 2, E])
        chosen = sb("chosen", [P, E], BF16)
        seen = sb("seen", [P, E], BF16)
        place = sb("place", [P, E])
        place2 = sb("place2", [P, 2, E])
        slotf = sb("slotf", [P, 2])
        slots = sb("slots", [P, 2, 2], I32)
        topv = sb("topv", [P, T, 2])
        ident = sb("ident", [P, P])
        tri = sb("tri", [P, P], BF16)
        ones_bf = sb("ones_bf", [P, P], BF16)
        mask32 = sb("mask32", [P, 32])
        mask = sb("mask", [P, GH])
        ones_pair = sb("ones_pair", [P, 2, 32])
        bout_sb = sb("bout_sb", [P, D])
        pos_sb = sb("pos_sb", [P, T, 2])
        ang = sb("ang", [P, 2, T, 2, 2])
        turns = sb("turns", [P, 2 * T * 4])
        cos_t = sb("cos_t", [P, T, 4])
        sin_t = sb("sin_t", [P, T, 2, 4])
        iota_e = sb("iota_e", [P, E])
        iota_ei = sb("iota_ei", [P, E], I32)
        region = sb("region", [P, E])
        dest_i = sb("dest_i", [P, T, 2], I32)
        dest = sb("dest", [P, T, 2])
        blk_dest = sb("blk_dest", [P, 2], I32)
        pad_row = sb("pad_row", [P, RW])
        wq_raw = sb("wq_raw", [P, KC, D])
        wkv_raw = sb("wkv_raw", [P, 2 * D])
        wq_p = sb("wq_p", [P, KC, D])
        wk_p = sb("wk_p", [P, D])
        wv_p = sb("wv_p", [P, 2, P])
        wout_sb = sb("wout_sb", [P, KC, D])
        wg_raw = sb("wg_raw", [E, D])
        wgT = sb("wgT", [P, KC, E])
        w1a = sb("w1a", [P, E, D])
        w1b = sb("w1b", [H - P, E, D])
        w12T = sb("w12T", [P, E, KC, 2 * H])
        w3_raw = sb("w3_raw", [P, KC, E, H])
        w3T = sb("w3T", [HA, E, 2, D])
        cntf = sb("cntf", [1, E])
        nblk = sb("nblk", [1, E])
        nblk2 = sb("nblk2", [1, E])
        blk_end = sb("blk_end", [1, E])
        onesrow = sb("onesrow", [1, E])
        jrow_i = sb("jrow_i", [1, NBLK], I32)
        jrow = sb("jrow", [1, NBLK])
        ended = sb("ended", [1, NBLK, E])
        ended_n = sb("ended_n", [1, NBLK, E])
        blk_exp = sb("blk_exp", [1, NBLK])
        blk_first = sb("blk_first", [1, NBLK])
        blk_row = sb("blk_row", [1, NBLK])
        blk_ecl = sb("blk_ecl", [1, NBLK])
        cnt_i = sb("cnt_i", [1, E], I32)
        exp_i = sb("exp_i", [1, NBLK], I32)
        row_i = sb("row_i", [1, NBLK], I32)
        xb = sb("xb", [P, 2, RW])
        xbT = sb("xbT", [P, 2, D])
        act_h = sb("act_h", [P, 2, H])
        gated = sb("gated", [P, 2, H])
        hT = sb("hT", [HA, 2, P])
        y_sb = sb("y_sb", [P, 2, D])
        wdiff = sb("wdiff", [P, T])
        wexp = sb("wexp", [P, T])
        wsum = sb("wsum", [P, T])
        wtop = sb("wtop", [P, 2, T])

        w_in = sem("w_in")
        wf1_in = sem("wf1_in")
        wf2_in = sem("wf2_in")
        wf3_in = sem("wf3_in")
        in_tile = [sem("in_even"), sem("in_odd")]
        pool_const = sem("pool_const")
        pool_step = sem("pool_step")
        dve_const = sem("dve_const")
        dve_step = sem("dve_step")
        rope_tables = sem("rope_tables")
        wt_done = sem("wt_done")
        waits_over = sem("waits_over")
        wt_sb = [sem("wt_sb_even"), sem("wt_sb_odd")]
        stats1_done, mv1_done, rstd1_done, xn_done, xb_done = (
            sem(s) for s in ("stats1_done", "mv1_done", "rstd1_done", "xn_done", "xb_done"))
        eps1_done, eps2_done = sem("eps1_done"), sem("eps2_done")
        xT_done, xT_sb, qk_done, v_done, v_sb = (sem(s) for s in ("xT_done", "xT_sb", "qk_done", "v_done", "v_sb"))
        rope_done, rot_done = sem("rope_done"), sem("rot_done")
        kT_done, kT_sb, qT_done, qT_sb, km_done = (sem(s) for s in ("kT_done", "kT_sb", "qT_done", "qT_sb", "km_done"))
        l_done, max_done, shift_done, exp_done, pt_done, pt_sb, pv_done = (
            sem(s) for s in ("l_done", "max_done", "shift_done", "exp_done", "pt_done", "pt_sb", "pv_done"))
        rden_done, norm_done, out_done, x1_done = (sem(s) for s in ("rden_done", "norm_done", "out_done", "x1_done"))
        stats2_done, mv2_done, rstd2_done, x2n_done = (
            sem(s) for s in ("stats2_done", "mv2_done", "rstd2_done", "x2n_done"))
        x2T_done, x2T_sb, gate_done, top_done, rank_done, rank_read, slot_done = (
            sem(s) for s in ("x2T_done", "x2T_sb", "gate_done", "top_done", "rank_done", "rank_read", "slot_done"))
        route_step = sem("route_step")
        chosen_done = sem("chosen_done")
        scattered = [sem("scattered_even"), sem("scattered_odd")]
        spare_in = sem("spare_in")
        cnt_done, tab_step, tab_done, pad_in = sem("cnt_done"), sem("tab_step"), sem("tab_done"), sem("pad_in")
        blk_in = [sem("blk_in_even"), sem("blk_in_odd")]
        bT_done, bT_sb, h_done, silu_done, gated_done, hT_done, hT_sb, y_done, y_copied = (
            sem(s) for s in ("bT_done", "bT_sb", "h_done", "silu_done", "gated_done", "hT_done", "hT_sb",
                             "y_done", "y_copied"))
        y_out = [sem("y_out_even"), sem("y_out_odd")]
        dest_done = sem("dest_done")
        wdiff_done, wexp_done, wtop_done = sem("wdiff_done"), sem("wexp_done"), sem("wtop_done")
        wg_done, wg_sb, w3_zero = sem("wg_done"), sem("wg_sb"), sem("w3_zero")
        y_back = [sem(f"y_back{n}") for n in range(4)]
        half_done, o_done = sem("half_done"), sem("o_done")
        o_stored = [sem(f"o_stored{n}") for n in range(4)]

        N_POOL_CONST, N_DVE_CONST, N_W = 9, 13, 6
        NWT = E * KC * 2 + E
        wt_banks = [banks[0], banks[1], banks[2], banks[3]]
        ps_h, ps_y, ps_hT = banks[0:2], banks[2:4], banks[4]
        w2a = km[:, 0].rearrange("p g h k -> p (g h k)").rearrange("p (e d) -> p e d", e=E)
        w2b = km[0:H - P, 1].rearrange("p g h k -> p (g h k)").rearrange("p (e d) -> p e d", e=E)
        y_in = pT[:].rearrange("p g (k d) -> p g k d", k=2)
        o_sb = expd[:].rearrange("p a (b d) -> p (a b) d", b=2)
        y_half = rope_a[:, 0:D]

        def weight_bank(n):
            if n < E * KC:
                return 1, n // KC, n % KC
            if n < E * KC + E:
                return 3, n - E * KC, 0
            n -= E * KC + E
            return 2, n // KC, n % KC

        def weight_copy(n):
            kind, e, c = weight_bank(n)
            ps = wt_banks[n % 4]
            if kind == 3:
                return w3T[:, e].rearrange("p c d -> p (c d)"), ps[0:HA, 0:2 * D]
            first = 0 if kind == 1 else H
            return w12T[:, e, c, first:first + H], ps[:, 0:H]

        block = es.enter_context(nc.Block())

        def apart(eng):
            eng.sem_inc(waits_over, 1)

        def wait_past(eng, semaphore, value):
            if not (isinstance(value, int) and value <= 0):
                eng.wait_ge(semaphore, value)

        def pipeline(eng, body):
            body(Tile(0, 0), True, False, True)
            body(Tile(0, 1), True, True, True)
            body(Tile(0, 2), True, True, True)
            with eng.Fori(1, (T - 4) // 2) as i:
                body(Tile(i, 1), True, True, True)
                body(Tile(i, 2), True, True, True)
            body(Tile(0, T - 3), True, True, True)
            body(Tile(0, T - 2), True, True, False)
            body(Tile(0, T - 1), False, True, False)

        @block.sync
        def _(sp):
            def load_tile(t):
                wait_past(sp, xn_done, t.n - 1)
                apart(sp)
                wait_past(sp, xT_done, t.n - 1)
                apart(sp)
                sp.dma_start(xres[:, bass.ds(t.n, 1), :].rearrange("p a d -> p (a d)"),
                             x_rows[bass.ds(t.times(P), P), :]).then_inc(in_tile[t.par], 16)
                sp.dma_start(ctx_sb[:, t.par, :], ctx_rows[bass.ds(t.times(P), P), :]).then_inc(in_tile[t.par], 16)

            load_tile(Tile(0, 0))
            sp.dma_start(wkv_raw[:], Wkv).then_inc(w_in, 16)
            sp.dma_start(wq_raw[:], Wq.rearrange("(c p) n -> p c n", p=P)).then_inc(w_in, 16)
            load_tile(Tile(0, 1))
            sp.dma_start(bout_sb[:], bout.rearrange("(a n) -> a n", a=1).broadcast_to([P, D])).then_inc(w_in, 16)
            sp.dma_start(wout_sb[:], Wout.rearrange("(c p) n -> p c n", p=P)).then_inc(w_in, 16)
            sp.dma_start(wg_raw[:], Wg).then_inc(w_in, 16)
            sp.dma_start(w1a[:], W1[:, 0:P, :].rearrange("e h d -> h e d")).then_inc(wf1_in, 16)
            sp.dma_start(w1b[:], W1[:, P:H, :].rearrange("e h d -> h e d")).then_inc(wf1_in, 16)
            for c in range(KC):
                sp.dma_start(w3_raw[:, c], W3[:, c * P:(c + 1) * P, :].rearrange("e p h -> p e h")).then_inc(wf3_in, 16)
            sp.wait_ge(pool_const, N_POOL_CONST)
            for s in range(SPARE):
                r0 = E * RC + s * P
                sp.dma_start(routed[r0:r0 + P, :], pad_row[:]).then_inc(spare_in, 16)
            with sp.Fori(1, T // 2) as i:
                load_tile(Tile(i, 0))
                load_tile(Tile(i, 1))

            sp.wait_ge(l_done, T * G)
            sp.dma_start(w2a, W2[:, 0:P, :].rearrange("e h d -> h e d")).then_inc(wf2_in, 16)
            sp.dma_start(w2b, W2[:, P:H, :].rearrange("e h d -> h e d")).then_inc(wf2_in, 16)
            sp.wait_ge(tab_done, 1)
            for e in range(E):
                n_e = sp.value_load(cnt_i[0:1, e:e + 1], min_val=0, max_val=TOKENS)
                sp.dma_start(routed[bass.ds(n_e + e * RC, P), :], pad_row[:]).then_inc(pad_in, 16)
            sp.wait_ge(pad_in, 16 * E)
            sp.wait_ge(spare_in, 16 * SPARE)
            for par in range(2):
                sp.wait_ge(scattered[par], 32 * (T // 2))

            def load_block(b):
                wait_past(sp, bT_done, b.n - 1)
                apart(sp)
                wait_past(sp, dest_done, b.n - 1)
                apart(sp)
                row = sp.value_load(row_i[0:1, bass.ds(b.n, 1)], min_val=0, max_val=E * RC + (SPARE - 1) * P)
                sp.dma_start(xb[:, b.par, :], routed[bass.ds(row, P), :]).then_inc(blk_in[b.par], 16)

            load_block(Tile(0, 0))
            load_block(Tile(0, 1))
            load_block(Tile(0, 2))
            with sp.Fori(1, (NBLK - 1) // 2) as i:
                load_block(Tile(i, 1))
                load_block(Tile(i, 2))

            sp.wait_ge(y_out[0], 16 * ((NBLK + 1) // 2))
            sp.wait_ge(y_out[1], 16 * (NBLK // 2))
            back = results.rearrange("(k r) d -> r k d", k=2)
            for u in range(4):
                sp.dma_start(y_in[:, u], back[u * P:(u + 1) * P]).then_inc(y_back[u], 16)
            with sp.Fori(1, T // 4) as i:
                for u in range(4):
                    sp.wait_ge(o_done, i * 4 + (u - 3))
                    apart(sp)
                    sp.dma_start(y_in[:, u], back[bass.ds(i * (4 * P) + u * P, P)]).then_inc(y_back[u], 16)

        @block.gpsimd
        def _(pool):
            nc.gpsimd.memset(minus_half[:], -0.5).then_inc(pool_const, 1)
            nc.gpsimd.memset(ident[:], 0.0).then_inc(pool_step, 1)
            nc.gpsimd.memset(mask32[:], 1.0).then_inc(pool_step, 1)
            nc.gpsimd.memset(tri[:], 1.0).then_inc(pool_step, 1)
            nc.gpsimd.memset(pad_row[:], 0.0).then_inc(pool_step, 1)
            pool.wait_ge(pool_step, 4)
            nc.gpsimd.affine_select(out=ident[:], in_=ident[:], compare_op=ALU.not_equal, fill=1.0, base=0,
                                    pattern=[[-1, P]], channel_multiplier=1).then_inc(pool_const, 1)
            nc.gpsimd.affine_select(out=mask32[:], in_=mask32[:], compare_op=ALU.is_ge, fill=0.0, base=0,
                                    pattern=[[-4, 32]], channel_multiplier=1).then_inc(pool_step, 1)
            pool.wait_ge(pool_step, 5)
            nc.gpsimd.affine_select(out=mask32[:], in_=mask32[:], compare_op=ALU.is_ge, fill=0.0, base=3,
                                    pattern=[[4, 32]], channel_multiplier=-1).then_inc(pool_const, 1)
            nc.gpsimd.affine_select(out=tri[:], in_=tri[:], compare_op=ALU.is_gt, fill=0.0, base=0,
                                    pattern=[[1, P]], channel_multiplier=-1).then_inc(pool_const, 1)
            nc.gpsimd.iota(dest_i[:], [[P, T], [TOKENS, 2]], base=0, channel_multiplier=1).then_inc(pool_const, 1)
            nc.gpsimd.iota(iota_ei[:], [[1, E]], base=0, channel_multiplier=0).then_inc(pool_const, 1)
            nc.gpsimd.iota(jrow_i[:], [[1, NBLK]], base=0, channel_multiplier=0).then_inc(pool_const, 1)
            nc.gpsimd.memset(pad_row[:, D:RW], float(NOWHERE)).then_inc(pool_const, 1)
            nc.gpsimd.memset(onesrow[:], 1.0).then_inc(pool_const, 1)

            def rstd_of_x(t):
                pool.wait_ge(mv1_done, t.n + 1)
                wait_past(pool, rstd1_done, t.n)
                apart(pool)
                nc.gpsimd.tensor_scalar(var_eps1[:], mv1[:, t.par, 1:2], EPS, None, ALU.add).then_inc(eps1_done, 1)
                pool.wait_ge(eps1_done, t.n + 1)
                wait_past(pool, xn_done, t.n - 1)
                nc.gpsimd.tensor_tensor(rstd1[:, t.par:t.par + 1], var_eps1[:], minus_half[:], ALU.pow)\
                    .then_inc(rstd1_done, 1)

            def rstd_of_x1(t):
                pool.wait_ge(mv2_done, t.n + 1)
                wait_past(pool, rstd2_done, t.n)
                apart(pool)
                nc.gpsimd.tensor_scalar(var_eps2[:], mv2[:, t.par, 1:2], EPS, None, ALU.add).then_inc(eps2_done, 1)
                pool.wait_ge(eps2_done, t.n + 1)
                wait_past(pool, x2n_done, t.times(3))
                nc.gpsimd.tensor_tensor(rstd2[:, t.par:t.par + 1], var_eps2[:], minus_half[:], ALU.pow)\
                    .then_inc(rstd2_done, 1)

            def add_bias(t):
                pool.wait_ge(w_in, 16 * N_W)
                pool.wait_ge(xn_done, t.n + 1)
                xt = xres[:, bass.ds(t.n, 1), :].rearrange("p a d -> p (a d)")
                nc.gpsimd.tensor_tensor(xt, xt, bout_sb[:], ALU.add).then_inc(xb_done, 1)

            def rotate(t):
                pool.wait_ge(rope_done, t.n + 1)
                pool.wait_ge(qT_done, t.n)
                nc.gpsimd.tensor_tensor(rot[:], rope_a[:], rope_b[:], ALU.add).then_inc(rot_done, 1)

            def mask_keys(t):
                pool.wait_ge(kT_sb, t.n + 1)
                wait_past(pool, l_done, t.times(G, -G))
                for g in range(G):
                    nc.gpsimd.tensor_tensor(km[:, t.par, g], kT[:, t.par, g].unsqueeze(1).broadcast_to([P, GH, N]),
                                            mask[:].unsqueeze(2).broadcast_to([P, GH, N]), ALU.mult)\
                        .then_inc(km_done, 1)

            def scatter(t):
                pool.wait_ge(slot_done, t.n + 1)
                apart(pool)
                for k in range(2):
                    nc.gpsimd.indirect_dma_start(
                        routed[:, :], bass.IndirectOffsetOnAxis(ap=slots[:, t.par, k:k + 1], axis=0),
                        xs[:, t.par, k, :], None).then_inc(scattered[t.par], 16)

            pool.wait_ge(dve_const, N_DVE_CONST)
            rstd_of_x(Tile(0, 0))
            rstd_of_x(Tile(0, 1))
            add_bias(Tile(0, 0))
            rotate(Tile(0, 0))
            mask_keys(Tile(0, 0))

            def body(t, front, back, ahead):
                if back:
                    rstd_of_x1(t.plus(-1))
                if front:
                    rotate(t.plus(1))
                if ahead:
                    rstd_of_x(t.plus(2))
                if front:
                    add_bias(t.plus(1))
                    mask_keys(t.plus(1))
                if back:
                    scatter(t.plus(-1))

            pipeline(pool, body)
            rstd_of_x1(Tile(0, T - 1))
            scatter(Tile(0, T - 1))

            def take_dest(b):
                pool.wait_ge(blk_in[b.par], b.half * 16 + 16)
                wait_past(pool, y_out[b.par], b.half * 16)
                apart(pool)
                nc.gpsimd.tensor_copy(blk_dest[:, b.par:b.par + 1], xb[:, b.par, D:RW]).then_inc(dest_done, 1)

            def store_block(b):
                pool.wait_ge(y_copied, b.n + 1)
                pool.wait_ge(dest_done, b.n + 1)
                apart(pool)
                nc.gpsimd.indirect_dma_start(
                    results[:, :], bass.IndirectOffsetOnAxis(ap=blk_dest[:, b.par:b.par + 1], axis=0),
                    y_sb[:, b.par, :], None, bounds_check=2 * TOKENS - 1, oob_is_err=False)\
                    .then_inc(y_out[b.par], 16)

            pool.wait_ge(wt_sb[0], NWT // 2)
            pool.wait_ge(wt_sb[1], NWT // 2)
            nc.gpsimd.memset(w3T[0:OVER, :, 1, :], 0.0).then_inc(w3_zero, 1)

            take_dest(Tile(0, 0))
            take_dest(Tile(0, 1))
            store_block(Tile(0, 0))
            for c in range(1, 3):
                take_dest(Tile(0, c + 1))
                store_block(Tile(0, c))
            with pool.Fori(1, (NBLK - 3) // 2) as i:
                for c in range(1, 3):
                    take_dest(Tile(i, c + 1))
                    store_block(Tile(i, c))
            take_dest(Tile(0, NBLK - 1))
            store_block(Tile(0, NBLK - 2))
            store_block(Tile(0, NBLK - 1))

        @block.vector
        def _(dve):
            V = nc.vector

            def stats_of_x(t):
                dve.wait_ge(in_tile[t.par], t.half * 32 + 32)
                wait_past(dve, mv1_done, t.n)
                apart(dve)
                V.bn_stats(stats[:, 0, :], xres[:, bass.ds(t.n, 1), :].rearrange("p a d -> p (a d)"))\
                    .then_inc(stats1_done, 1)
                dve.wait_ge(stats1_done, t.n + 1)
                wait_past(dve, xn_done, t.n - 1)
                apart(dve)
                V.bn_aggr(mv1[:, t.par, :], stats[:, 0, :]).then_inc(mv1_done, 1)

            def normalise_x(t):
                dve.wait_ge(rstd1_done, t.n + 1)
                wait_past(dve, xT_done, t.n - 1)
                V.tensor_scalar(xn[:, t.par, :], xres[:, bass.ds(t.n, 1), :].rearrange("p a d -> p (a d)"),
                                mv1[:, t.par, 0:1], rstd1[:, t.par:t.par + 1], ALU.subtract, ALU.mult)\
                    .then_inc(xn_done, 1)

            def rope(t):
                dve.wait_ge(qk_done, t.n + 1)
                dve.wait_ge(rot_done, t.n)
                cos = cos_t[:, bass.ds(t.n, 1), :].rearrange("p a c -> p (a c)")
                V.tensor_tensor(rope_a[:].rearrange("p (s c) -> p s c", c=4),
                                ps_qk[:].rearrange("p (s c) -> p s c", c=4),
                                cos.unsqueeze(1).broadcast_to([P, P, 4]), ALU.mult)
                for i in range(2):
                    sn = sin_t[:, bass.ds(t.n, 1), i, :].rearrange("p a c -> p (a c)")
                    o = rope_b[:].rearrange("p (s i h c) -> p s i h c", s=2 * G, i=2, c=4)[:, :, i]
                    q = ps_qk[:].rearrange("p (s i h c) -> p s i h c", s=2 * G, i=2, c=4)[:, :, 1 - i]
                    ins = V.tensor_tensor(o, q, sn.unsqueeze(1).unsqueeze(1).broadcast_to([P, 2 * G, GH, 4]), ALU.mult)
                ins.then_inc(rope_done, 1)

            def shift(t, g):
                l = ps_l[g % 2][:].rearrange("p (h k) -> p h k", k=N)
                dve.wait_ge(l_done, t.times(G, g + 1))
                wait_past(dve, shift_done, t.times(G, g - 1))
                V.tensor_reduce(rowmax[:, g % 2, :], l, AX_X, ALU.max).then_inc(max_done, 1)
                dve.wait_ge(max_done, t.times(G, g + 1))
                wait_past(dve, exp_done, t.times(G, g - 1))
                V.tensor_tensor(shifted[:, g % 2, :].rearrange("p (h k) -> p h k", k=N), l,
                                rowmax[:, g % 2, :].unsqueeze(2).broadcast_to([P, GH, N]), ALU.subtract)\
                    .then_inc(shift_done, 1)

            def normalise_attn(t):
                dve.wait_ge(pv_done, t.times(2, 2))
                wait_past(dve, norm_done, t.n)
                V.reciprocal(rden[:], ps_nd[:, D:2 * D]).then_inc(rden_done, 1)
                dve.wait_ge(rden_done, t.n + 1)
                dve.wait_ge(out_done, t.n)
                V.tensor_tensor(attnT[:], ps_nd[:, 0:D], rden[:], ALU.mult).then_inc(norm_done, 1)

            def residual(t):
                xt = xres[:, bass.ds(t.n, 1), :].rearrange("p a d -> p (a d)")
                dve.wait_ge(out_done, t.n + 1)
                dve.wait_ge(xb_done, t.n + 1)
                V.tensor_tensor(xt, ps_vo[:, 0:D], xt, ALU.add).then_inc(x1_done, 1)
                dve.wait_ge(x1_done, t.n + 1)
                wait_past(dve, mv2_done, t.n)
                apart(dve)
                V.bn_stats(stats[:, 1, :], xt).then_inc(stats2_done, 1)
                dve.wait_ge(stats2_done, t.n + 1)
                wait_past(dve, x2n_done, t.times(3))
                apart(dve)
                V.bn_aggr(mv2[:, t.par, :], stats[:, 1, :]).then_inc(mv2_done, 1)

            def normalise_x1(t):
                xt = xres[:, bass.ds(t.n, 1), :].rearrange("p a d -> p (a d)")
                dve.wait_ge(rstd2_done, t.n + 1)
                dve.wait_ge(scattered[t.par], t.half * 32)
                dve.wait_ge(x2T_done, t.n)
                for k in range(2):
                    V.tensor_scalar(xs[:, t.par, k, 0:D], xt, mv2[:, t.par, 0:1], rstd2[:, t.par:t.par + 1],
                                    ALU.subtract, ALU.mult).then_inc(x2n_done, 1)
                V.tensor_copy(xs[:, t.par, :, D:RW],
                              dest[:, bass.ds(t.n, 1), :].rearrange("p a k -> p (a k)").unsqueeze(2))\
                    .then_inc(x2n_done, 1)

            def choose(t):
                scores = ps_tr[:, 0:E]
                dve.wait_ge(gate_done, t.n + 1)
                wait_past(dve, slot_done, t.n)
                apart(dve)
                V.max(top8[:], scores).then_inc(route_step, 1)
                dve.wait_ge(route_step, t.times(6, 1))
                apart(dve)
                V.max_index(idx8[:], top8[:], scores).then_inc(route_step, 1)
                V.tensor_copy(topv[:, bass.ds(t.n, 1), :].rearrange("p a k -> p (a k)"), top8[:, 0:2])
                dve.wait_ge(route_step, t.times(6, 2))
                V.tensor_copy(idxf[:], idx8[:, 0:2]).then_inc(route_step, 1)
                dve.wait_ge(route_step, t.times(6, 3))
                V.tensor_tensor(onehot[:], iota_e[:].unsqueeze(1).broadcast_to([P, 2, E]),
                                idxf[:].unsqueeze(2).broadcast_to([P, 2, E]), ALU.is_equal).then_inc(route_step, 1)
                dve.wait_ge(route_step, t.times(6, 4))
                dve.wait_ge(rank_done, t.n)
                V.tensor_tensor(chosen[:], onehot[:, 0, :], onehot[:, 1, :], ALU.add).then_inc(top_done, 1)

            def allot(t):
                dve.wait_ge(rank_done, t.n + 1)
                wait_past(dve, chosen_done, t.n)
                V.tensor_tensor(place[:], ps_tr[:, E:2 * E], region[:], ALU.add).then_inc(rank_read, 1)
                V.tensor_tensor(seen[:], seen[:], chosen[:], ALU.add).then_inc(chosen_done, 1)
                dve.wait_ge(rank_read, t.n + 1)
                V.tensor_tensor(place2[:], onehot[:], place[:].unsqueeze(1).broadcast_to([P, 2, E]), ALU.mult)\
                    .then_inc(route_step, 1)
                dve.wait_ge(route_step, t.times(6, 5))
                V.tensor_reduce(slotf[:], place2[:], AX_X, ALU.add).then_inc(route_step, 1)
                dve.wait_ge(route_step, t.times(6, 6))
                V.tensor_copy(slots[:, t.par, :], slotf[:]).then_inc(slot_done, 1)

            steps = [0]

            def step(ins):
                steps[0] += 1
                ins.then_inc(dve_step, 1)
                dve.wait_ge(dve_step, steps[0])

            V.memset(qbd[:], 0.0).then_inc(dve_const, 1)
            V.memset(vst[:], 0.0).then_inc(dve_const, 1)
            V.memset(seen[:], 0.0).then_inc(dve_const, 1)
            V.memset(ones_bf[:], 1.0).then_inc(dve_const, 1)
            step(V.memset(ones_pair[:], 0.0))
            for par in range(2):
                for h in range(2):
                    ins = V.memset(ones_pair[64 * h:64 * h + 64, par, 16 * par + 8 * h:16 * par + 8 * h + 8], 1.0)
            ins.then_inc(dve_const, 1)
            stats_of_x(Tile(0, 0))
            stats_of_x(Tile(0, 1))
            dve.wait_ge(pool_const, N_POOL_CONST)
            V.tensor_reduce(mask[:], mask32[:].rearrange("p (a h) -> p h a", h=GH), AX_X, ALU.add)\
                .then_inc(dve_const, 1)
            step(V.tensor_copy(iota_e[:], iota_ei[:]))
            V.tensor_scalar(region[:], iota_e[:], float(RC), None, ALU.mult).then_inc(dve_const, 1)
            V.tensor_copy(jrow[:], jrow_i[:]).then_inc(dve_const, 1)
            V.tensor_copy(dest[:], dest_i[:]).then_inc(dve_const, 1)
            dve.wait_ge(w_in, 16 * N_W)
            for c in range(KC):
                V.tensor_copy(wq_p[:, c].rearrange("p (g i m) -> p g i m", g=G, i=2),
                              wq_raw[:, c].rearrange("p (g m i) -> p g i m", g=G, i=2)).then_inc(dve_const, 1)
            V.tensor_copy(wk_p[:].rearrange("p (g i m) -> p g i m", g=G, i=2),
                          wkv_raw[:, 0:D].rearrange("p (g m i) -> p g i m", g=G, i=2)).then_inc(dve_const, 1)
            V.tensor_copy(wv_p[:].rearrange("p o (h d) -> p o h d", d=HD),
                          wkv_raw[:, D:2 * D].rearrange("p (h o d) -> p o h d", o=2, d=HD)).then_inc(dve_const, 1)
            normalise_x(Tile(0, 0))
            normalise_x(Tile(0, 1))
            step(V.tensor_copy(ang[:, 0, :, :, 0], pos_sb[:]))
            step(V.tensor_scalar(ang[:, 0, :, :, 1], pos_sb[:], 10000.0 ** -0.5, None, ALU.mult))
            step(V.tensor_scalar(ang[:, 1], ang[:, 0], math.pi / 2, None, ALU.add))
            af = ang[:].rearrange("p a t c h -> p (a t c h)")
            step(V.tensor_scalar(turns[:], af, 1 / (2 * math.pi), MAGIC, ALU.mult, ALU.add))
            step(V.tensor_scalar(turns[:], turns[:], MAGIC, None, ALU.subtract))
            step(V.scalar_tensor_tensor(af, turns[:], -6.28125, af, ALU.mult, ALU.add))
            step(V.scalar_tensor_tensor(af, turns[:], -(2 * math.pi - 6.28125), af, ALU.mult, ALU.add))
            V.tensor_scalar(af, af, 3.1415925, -3.1415925, ALU.min, ALU.max).then_inc(rope_tables, 1)
            dve.wait_ge(rope_tables, 4)
            rope(Tile(0, 0))

            def body(t, front, back, ahead):
                shift(t, 0)
                shift(t, 1)
                if back:
                    residual(t.plus(-1))
                shift(t, 2)
                if back:
                    normalise_x1(t.plus(-1))
                if front:
                    rope(t.plus(1))
                if ahead:
                    stats_of_x(t.plus(2))
                shift(t, 3)
                if back:
                    choose(t.plus(-1))
                if ahead:
                    normalise_x(t.plus(2))
                if back:
                    allot(t.plus(-1))
                normalise_attn(t)

            pipeline(dve, body)
            residual(Tile(0, T - 1))
            normalise_x1(Tile(0, T - 1))
            choose(Tile(0, T - 1))
            allot(Tile(0, T - 1))

            dve.wait_ge(cnt_done, 1)
            tabs = [0]

            def tab(ins):
                tabs[0] += 1
                ins.then_inc(tab_step, 1)
                dve.wait_ge(tab_step, tabs[0])

            tab(V.tensor_copy(cntf[:], ps_vo[0:1, 0:E]))
            V.tensor_copy(cnt_i[:], cntf[:])
            tab(V.tensor_scalar(nblk[:], cntf[:], 1.0 / P, (P - 1) / P - 0.5 + 0.5 / P, ALU.mult, ALU.add))
            tab(V.tensor_scalar(nblk[:], nblk[:], MAGIC, None, ALU.add))
            tab(V.tensor_scalar(nblk2[:], nblk[:], MAGIC, None, ALU.subtract))
            tab(V.tensor_tensor_scan(blk_end[:], onesrow[:], nblk2[:], 0.0, ALU.mult, ALU.add))
            je = [1, NBLK, E]
            tab(V.tensor_tensor(ended[:], jrow[:].unsqueeze(2).broadcast_to(je),
                                blk_end[:].unsqueeze(1).broadcast_to(je), ALU.is_ge))
            tab(V.tensor_tensor(ended_n[:], ended[:], nblk2[:].unsqueeze(1).broadcast_to(je), ALU.mult))
            tab(V.tensor_reduce(blk_exp[:], ended[:], AX_X, ALU.add))
            tab(V.tensor_reduce(blk_first[:], ended_n[:], AX_X, ALU.add))
            tab(V.tensor_tensor(blk_row[:], jrow[:], blk_first[:], ALU.subtract))
            tab(V.tensor_scalar(blk_row[:], blk_row[:], float(P), None, ALU.mult))
            tab(V.scalar_tensor_tensor(blk_row[:], blk_exp[:], float(RC), blk_row[:], ALU.mult, ALU.add))
            tab(V.tensor_scalar(blk_ecl[:], blk_exp[:], float(E - 1), None, ALU.min))
            V.tensor_copy(exp_i[:], blk_ecl[:])
            V.tensor_tensor(wdiff[:], topv[:, :, 1], topv[:, :, 0], ALU.subtract).then_inc(wdiff_done, 1)
            V.tensor_copy(row_i[:], blk_row[:]).then_inc(tab_done, 1)

            for n in range(1, NWT, 2):
                dve.wait_ge(wt_done, n + 1)
                into, ps = weight_copy(n)
                V.tensor_copy(into, ps).then_inc(wt_sb[1], 1)
            dve.wait_ge(wexp_done, 1)
            V.tensor_scalar(wsum[:], wexp[:], 1.0, None, ALU.add).then_inc(wtop_done, 1)
            dve.wait_ge(wtop_done, 1)
            V.reciprocal(wtop[:, 0, :], wsum[:]).then_inc(wtop_done, 1)
            dve.wait_ge(wtop_done, 2)
            V.tensor_tensor(wtop[:, 1, :], wexp[:], wtop[:, 0, :], ALU.mult).then_inc(wtop_done, 1)

            def gate(b):
                dve.wait_ge(silu_done, b.n + 1)
                wait_past(dve, hT_done, b.n - 1)
                V.tensor_tensor(gated[:, b.par, :], act_h[:, b.par, :], ps_h[b.par][:, H:2 * H], ALU.mult)\
                    .then_inc(gated_done, 1)

            def copy_hT(b):
                dve.wait_ge(hT_done, b.n + 1)
                dve.wait_ge(y_done, b.n)
                V.tensor_copy(hT[:].rearrange("p c t -> p (c t)"), ps_hT[0:HA, 0:2 * P]).then_inc(hT_sb, 1)

            def copy_y(b):
                dve.wait_ge(y_done, b.n + 1)
                dve.wait_ge(y_out[b.par], b.half * 16)
                V.tensor_copy(y_sb[:, b.par, :], ps_y[b.par][:, 0:D]).then_inc(y_copied, 1)

            def ffn_body(b, before):
                gate(b)
                if before:
                    copy_y(b.plus(-1))
                copy_hT(b)

            ffn_body(Tile(0, 0), False)
            ffn_body(Tile(0, 1), True)
            ffn_body(Tile(0, 2), True)
            with dve.Fori(1, (NBLK - 1) // 2) as i:
                ffn_body(Tile(i, 1), True)
                ffn_body(Tile(i, 2), True)
            copy_y(Tile(0, NBLK - 1))

            def combine(i, u):
                t = i * 4 + u
                dve.wait_ge(y_back[u], i * 16 + 16)
                wait_past(dve, o_done, t)
                V.scalar_tensor_tensor(y_half, y_in[:, u, 0, :], wtop[:, 0, bass.ds(t, 1)],
                                       xres[:, bass.ds(t, 1), :].rearrange("p a d -> p (a d)"),
                                       ALU.mult, ALU.add).then_inc(half_done, 1)
                dve.wait_ge(half_done, t + 1)
                wait_past(dve, o_stored[u], i * 16)
                V.scalar_tensor_tensor(o_sb[:, u, :], y_in[:, u, 1, :], wtop[:, 1, bass.ds(t, 1)], y_half,
                                       ALU.mult, ALU.add).then_inc(o_done, 1)

            for u in range(4):
                combine(0, u)
            with dve.Fori(1, T // 4) as i:
                for u in range(4):
                    combine(i, u)

        @block.scalar
        def _(act):
            S = nc.scalar

            def copy_xT(t):
                act.wait_ge(xT_done, t.n + 1)
                act.wait_ge(v_done, t.n)
                S.activation(xT[:], ps_tr[:, 0:3 * P], ACT.Copy).then_inc(xT_sb, 1)

            def copy_v(t):
                act.wait_ge(v_done, t.n + 1)
                wait_past(act, pv_done, t.times(2, -2))
                for o in range(2):
                    into = vst[64 * o:64 * o + 64, t.par].rearrange("p (j q) c -> p j q c", q=2)
                    for q in range(2):
                        ins = S.activation(into[:, :, q, 16 * q + 8 * o:16 * q + 8 * o + 8],
                                           ps_vo[64 * o:64 * o + 64, D:2 * D].rearrange(
                                               "p (j q d) -> p j q d", q=2, d=HD)[:, :, q], ACT.Copy)
                ins.then_inc(v_sb, 1)

            def copy_kT(t):
                act.wait_ge(kT_done, t.n + 1)
                wait_past(act, km_done, t.times(G, -G))
                for b in range(2):
                    ins = S.activation(kT[64 * b:64 * b + 64, t.par], ps_tr[0:64, :].rearrange(
                        "p (g b k) -> p g b k", g=G, b=2)[:, :, b], ACT.Copy)
                ins.then_inc(kT_sb, 1)

            def copy_qT(t):
                act.wait_ge(qT_done, t.n + 1)
                wait_past(act, l_done, t.times(G, -G))
                for b in range(2):
                    ins = S.activation(qbd[64 * b:64 * b + 64, t.par, :, 64 * b:64 * b + 64], ps_tr[0:64, :].rearrange(
                        "p (g b k) -> p g b k", g=G, b=2)[:, :, b], ACT.Copy)
                ins.then_inc(qT_sb, 1)

            def exponential(t, g):
                act.wait_ge(shift_done, t.times(G, g + 1))
                wait_past(act, pt_done, t.times(G, g - 1))
                S.activation(expd[:, g % 2, :], shifted[:, g % 2, :], ACT.Exp, scale=SCALE).then_inc(exp_done, 1)

            def copy_pT(t, g):
                act.wait_ge(pt_done, t.times(G, g + 1))
                wait_past(act, pv_done, t.times(2, g // 2 - 1))
                S.activation(pT[:, g, :], ps_pt[g % 2][:], ACT.Copy).then_inc(pt_sb, 1)

            def copy_x2T(t):
                act.wait_ge(x2T_done, t.n + 1)
                act.wait_ge(gate_done, t.n)
                S.activation(x2T[:], ps_tr[:, 0:D], ACT.Copy).then_inc(x2T_sb, 1)

            act.dma_start(pos_sb[:], pos_rows).then_inc(w_in, 16)
            act.wait_ge(rope_tables, 1)
            af = ang[:].rearrange("p a t c h -> p a t (c h)")
            S.activation(sin_t[:, :, 0, :], af[:, 0], ACT.Sin, scale=-1.0).then_inc(rope_tables, 1)
            S.activation(sin_t[:, :, 1, :], af[:, 0], ACT.Sin).then_inc(rope_tables, 1)
            S.activation(cos_t[:], af[:, 1], ACT.Sin).then_inc(rope_tables, 1)
            act.wait_ge(wg_done, 1)
            S.activation(wgT[:], ps_nd[:, 0:KC * E].rearrange("p (c e) -> p c e", c=KC), ACT.Copy)\
                .then_inc(wg_sb, 1)
            act.wait_ge(dve_const, N_DVE_CONST)
            copy_xT(Tile(0, 0))
            copy_v(Tile(0, 0))
            copy_kT(Tile(0, 0))
            copy_qT(Tile(0, 0))

            def body(t, front, back, ahead):
                exponential(t, 0)
                if front:
                    copy_xT(t.plus(1))
                exponential(t, 1)
                copy_pT(t, 0)
                if front:
                    copy_v(t.plus(1))
                exponential(t, 2)
                copy_pT(t, 1)
                if back:
                    copy_x2T(t.plus(-1))
                copy_pT(t, 2)
                exponential(t, 3)
                if front:
                    copy_kT(t.plus(1))
                copy_pT(t, 3)
                if front:
                    copy_qT(t.plus(1))

            pipeline(act, body)
            copy_x2T(Tile(0, T - 1))

            for n in range(0, NWT, 2):
                act.wait_ge(wt_done, n + 1)
                into, ps = weight_copy(n)
                S.activation(into, ps, ACT.Copy).then_inc(wt_sb[0], 1)
            act.wait_ge(wdiff_done, 1)
            S.activation(wexp[:], wdiff[:], ACT.Exp).then_inc(wexp_done, 1)

            def copy_xbT(b):
                act.wait_ge(bT_done, b.n + 1)
                wait_past(act, h_done, b.n - 1)
                S.activation(xbT[:, b.par, :], ps_tr[:, 0:D], ACT.Copy).then_inc(bT_sb, 1)

            def silu(b):
                act.wait_ge(h_done, b.n + 1)
                wait_past(act, gated_done, b.n - 1)
                S.activation(act_h[:, b.par, :], ps_h[b.par][:, 0:H], ACT.Silu).then_inc(silu_done, 1)

            copy_xbT(Tile(0, 0))
            silu(Tile(0, 0))
            copy_xbT(Tile(0, 1))
            for c in range(1, 3):
                silu(Tile(0, c))
                copy_xbT(Tile(0, c + 1))
            with act.Fori(1, (NBLK - 3) // 2) as i:
                for c in range(1, 3):
                    silu(Tile(i, c))
                    copy_xbT(Tile(i, c + 1))
            silu(Tile(0, NBLK - 2))
            copy_xbT(Tile(0, NBLK - 1))
            silu(Tile(0, NBLK - 1))

            with act.Fori(0, T // 4) as i:
                for u in range(4):
                    act.wait_ge(o_done, i * 4 + (u + 1))
                    act.dma_start(out_rows[bass.ds(i * (4 * P) + u * P, P), :], o_sb[:, u, :])\
                        .then_inc(o_stored[u], 16)
            for u in range(4):
                act.wait_ge(o_stored[u], 16 * (T // 4))

        @block.tensor
        def _(pe):
            M = nc.tensor

            def transpose_x(t):
                pe.wait_ge(xn_done, t.n + 1)
                pe.wait_ge(in_tile[t.par], t.half * 32 + 32)
                pe.wait_ge(qT_sb, t.n)
                for c in range(KC):
                    M.transpose(ps_tr[:, c * P:(c + 1) * P], xn[:, t.par, c * P:(c + 1) * P], ident[:])
                M.transpose(ps_tr[:, D:D + P], ctx_sb[:, t.par, :], ident[:]).then_inc(xT_done, 1)

            def project(t):
                pe.wait_ge(xT_sb, t.n + 1)
                pe.wait_ge(rope_done, t.n)
                for c in range(KC):
                    M.matmul(ps_qk[:, 0:D], xT[:, c * P:(c + 1) * P], wq_p[:, c, :], start=(c == 0), stop=(c == KC - 1))
                M.matmul(ps_qk[:, D:2 * D], xT[:, D:D + P], wk_p[:], start=True, stop=True).then_inc(qk_done, 1)
                wait_past(pe, x1_done, t.n - 1)
                for b in range(2):
                    for o in range(2):
                        ins = M.matmul(ps_vo[64 * o:64 * o + 64, D + b * P:D + (b + 1) * P],
                                       xT[:, D + 64 * b:D + 64 * b + 64], wv_p[:, o, :], start=True, stop=True)
                ins.then_inc(v_done, 1)

            def transpose_rot(t, first, ready, done):
                pe.wait_ge(*ready)
                apart(pe)
                for g in range(G):
                    ins = M.transpose(ps_tr[0:GW, g * P:(g + 1) * P], rot[:, first + g * GW:first + (g + 1) * GW],
                                      ident[:])
                ins.then_inc(done, 1)

            def transpose_k(t):
                pe.wait_ge(rot_done, t.n + 1)
                transpose_rot(t, D, (rank_read, t.n - 1) if not (isinstance(t.i, int) and t.n < 2)
                              else (xT_sb, t.n + 1), kT_done)

            def transpose_q(t):
                transpose_rot(t, 0, (kT_sb, t.n + 1), qT_done)

            def logits(t, g):
                pe.wait_ge(km_done, t.times(G, g + 1))
                if g == 0:
                    pe.wait_ge(qT_sb, t.n + 1)
                wait_past(pe, shift_done, t.times(G, g - 1))
                M.matmul(ps_l[g % 2][:], qbd[:, t.par, g, :], km[:, t.par, g].rearrange("p h k -> p (h k)"),
                         start=True, stop=True).then_inc(l_done, 1)

            def transpose_p(t, g):
                pe.wait_ge(exp_done, t.times(G, g + 1))
                wait_past(pe, pt_sb, t.times(G, g - 1))
                for j in range(G):
                    ins = M.transpose(ps_pt[g % 2][:, j * P:(j + 1) * P], expd[:, g % 2, j * P:(j + 1) * P], ident[:])
                ins.then_inc(pt_done, 1)

            def attend(t, c):
                pe.wait_ge(pt_sb, t.times(G, 2 * c + 2))
                if c == 0:
                    pe.wait_ge(v_sb, t.n + 1)
                    pe.wait_ge(norm_done, t.n)
                probs = pT[:].rearrange("p g (j k) -> p (g j) k", k=P)
                for b in range(2):
                    for q in range(2):
                        for j in range(4):
                            pair = 8 * c + 2 * j + q
                            M.matmul(ps_nd[32 * j:32 * j + 32, c * P + 64 * b:c * P + 64 * b + 64],
                                     vst[:, t.par, 16 * b + pair, :], probs[:, pair, 64 * b:64 * b + 64],
                                     start=(q == 0), stop=(q == 1))
                for q in range(2):
                    for j in range(4):
                        ins = M.matmul(ps_nd[32 * j:32 * j + 32, D + c * P:D + (c + 1) * P], ones_pair[:, q, :],
                                       probs[:, 8 * c + 2 * j + q, :], start=(q == 0), stop=(q == 1))
                ins.then_inc(pv_done, 1)

            def project_out(t, v_copied):
                pe.wait_ge(norm_done, t.n + 1)
                pe.wait_ge(v_sb, v_copied)
                for c in range(KC):
                    ins = M.matmul(ps_vo[:, 0:D], attnT[:, c * P:(c + 1) * P], wout_sb[:, c, :],
                                   start=(c == 0), stop=(c == KC - 1))
                ins.then_inc(out_done, 1)

            def transpose_x1(t, x_copied):
                pe.wait_ge(x2n_done, t.times(3, 3))
                pe.wait_ge(*x_copied)
                for c in range(KC):
                    ins = M.transpose(ps_tr[:, c * P:(c + 1) * P], xs[:, t.par, 0, c * P:(c + 1) * P], ident[:])
                ins.then_inc(x2T_done, 1)

            def score(t):
                pe.wait_ge(x2T_sb, t.n + 1)
                for c in range(KC):
                    ins = M.matmul(ps_tr[:, 0:E], x2T[:, c * P:(c + 1) * P], wgT[:, c, :],
                                   start=(c == 0), stop=(c == KC - 1))
                ins.then_inc(gate_done, 1)

            def rank(t):
                pe.wait_ge(top_done, t.n + 1)
                pe.wait_ge(chosen_done, t.n)
                M.matmul(ps_tr[:, E:2 * E], tri[:], chosen[:], start=True, stop=False)
                M.matmul(ps_tr[:, E:2 * E], ones_bf[:], seen[:], start=False, stop=True).then_inc(rank_done, 1)

            pe.wait_ge(pool_const, N_POOL_CONST)
            pe.wait_ge(w_in, 16 * N_W)
            for c in range(KC):
                ins = M.transpose(ps_nd[:, c * E:(c + 1) * E], wg_raw[:, c * P:(c + 1) * P], ident[0:E, 0:E])
            ins.then_inc(wg_done, 1)
            pe.wait_ge(wg_sb, 1)
            pe.wait_ge(dve_const, N_DVE_CONST)
            transpose_x(Tile(0, 0))
            project(Tile(0, 0))
            transpose_k(Tile(0, 0))
            transpose_q(Tile(0, 0))

            def body(t, front, back, ahead):
                logits(t, 0)
                logits(t, 1)
                if back:
                    project_out(t.plus(-1), t.n + 1)
                if front:
                    transpose_x(t.plus(1))
                transpose_p(t, 0)
                logits(t, 2)
                if front:
                    project(t.plus(1))
                transpose_p(t, 1)
                logits(t, 3)
                if back:
                    transpose_x1(t.plus(-1), (xT_sb, t.n + 2) if front else (qT_sb, t.n + 1))
                transpose_p(t, 2)
                if back:
                    score(t.plus(-1))
                attend(t, 0)
                if back:
                    rank(t.plus(-1))
                if front:
                    transpose_k(t.plus(1))
                transpose_p(t, 3)
                if front:
                    transpose_q(t.plus(1))
                attend(t, 1)

            pipeline(pe, body)
            project_out(Tile(0, T - 1), T)
            transpose_x1(Tile(0, T - 1), (rank_read, T - 1))
            score(Tile(0, T - 1))
            rank(Tile(0, T - 1))
            pe.wait_ge(chosen_done, T)
            pe.wait_ge(x1_done, T)
            M.matmul(ps_vo[:, 0:E], ones_bf[:], seen[:], start=True, stop=True).then_inc(cnt_done, 1)

            for n in range(NWT):
                kind, e, c = weight_bank(n)
                if n == 0:
                    pe.wait_ge(shift_done, T * G)
                    pe.wait_ge(pt_sb, T * G)
                    pe.wait_ge(wf1_in, 32)
                if n == E * KC:
                    pe.wait_ge(wf3_in, 32)
                if n == E * KC + E:
                    pe.wait_ge(wf2_in, 32)
                if n >= 4:
                    pe.wait_ge(wt_sb[n % 2], (n - 4) // 2 + 1)
                ps = wt_banks[n % 4]
                if kind == 3:
                    for h in range(2):
                        for d in range(KC):
                            ins = M.transpose(ps[0:HA, h * D + d * P:h * D + (d + 1) * P],
                                              w3_raw[:, d, e, h * HB:h * HB + HA], ident[:])
                else:
                    wa, wb = (w1a[:], w1b[:]) if kind == 1 else (w2a, w2b)
                    M.transpose(ps[:, 0:P], wa[:, e, c * P:(c + 1) * P], ident[:])
                    ins = M.transpose(ps[:, P:H], wb[:, e, c * P:(c + 1) * P], ident[0:H - P, 0:H - P])
                ins.then_inc(wt_done, 1)

            def transpose_block(b):
                pe.wait_ge(blk_in[b.par], b.half * 16 + 16)
                pe.wait_ge(bT_sb, b.n)
                for c in range(KC):
                    ins = M.transpose(ps_tr[:, c * P:(c + 1) * P], xb[:, b.par, c * P:(c + 1) * P], ident[:])
                ins.then_inc(bT_done, 1)

            def hidden(b, e):
                pe.wait_ge(bT_sb, b.n + 1)
                wait_past(pe, gated_done, b.n - 1)
                for c in range(KC):
                    ins = M.matmul(ps_h[b.par][:, 0:2 * H], xbT[:, b.par, c * P:(c + 1) * P],
                                   w12T[:, bass.ds(e, 1), c, :].rearrange("p a h -> p (a h)"),
                                   start=(c == 0), stop=(c == KC - 1))
                ins.then_inc(h_done, 1)

            def transpose_hidden(b):
                pe.wait_ge(gated_done, b.n + 1)
                pe.wait_ge(hT_sb, b.n)
                for c in range(2):
                    ins = M.transpose(ps_hT[0:HA, c * P:(c + 1) * P], gated[:, b.par, c * HB:c * HB + HA], ident[:])
                ins.then_inc(hT_done, 1)

            def result(b, e):
                pe.wait_ge(hT_sb, b.n + 1)
                wait_past(pe, y_copied, b.n - 1)
                for c in range(2):
                    ins = M.matmul(ps_y[b.par][:, 0:D], hT[:, c, :],
                                   w3T[:, bass.ds(e, 1), c, :].rearrange("p a d -> p (a d)"),
                                   start=(c == 0), stop=(c == 1))
                ins.then_inc(y_done, 1)

            def expert_of(b):
                return pe.value_load(exp_i[0:1, bass.ds(b.n, 1)], min_val=0, max_val=E - 1)

            pe.wait_ge(tab_done, 1)
            pe.wait_ge(wt_sb[0], NWT // 2)
            pe.wait_ge(w3_zero, 1)
            def ffn_body(b, before=True, after=True):
                hidden(b, expert_of(b))
                if after:
                    transpose_block(b.plus(1))
                if before:
                    result(b.plus(-1), expert_of(b.plus(-1)))
                transpose_hidden(b)

            transpose_block(Tile(0, 0))
            ffn_body(Tile(0, 0), before=False)
            ffn_body(Tile(0, 1))
            ffn_body(Tile(0, 2))
            with pe.Fori(1, (NBLK - 3) // 2) as i:
                ffn_body(Tile(i, 1))
                ffn_body(Tile(i, 2))
            ffn_body(Tile(0, NBLK - 2))
            ffn_body(Tile(0, NBLK - 1), after=False)
            result(Tile(0, NBLK - 1), expert_of(Tile(0, NBLK - 1)))
    return nc


_INS = ['x', 'ctx_1024', 'fside_BxSx2_0', 'L0_xattn_Wq', 'L0_xattn_Wkv', 'L0_xattn_Wout', 'L0_xattn_bout',
        'L0_ffn_Wg', 'L0_ffn_W1', 'L0_ffn_W2', 'L0_ffn_W3']


def kernel(**inputs):
    import numpy as _np
    import concourse.bacc as _bacc
    from concourse import mybir as _mybir
    from concourse.bass_utils import run_bass_kernel_spmd as _run

    nc = _bacc.Bacc("TRN2", target_bir_lowering=False, num_devices=1)
    arrays, args = {}, []
    for name in _INS:
        a = _np.ascontiguousarray(inputs[name])
        arrays[f"in_{name}_dram"] = a
        args.append(nc.dram_tensor(f"in_{name}_dram", a.shape, _mybir.dt.from_np(a.dtype), kind="ExternalInput").ap())
    args.append(nc.dram_tensor("out_0_dram", (64, 64, 256), _mybir.dt.float32, kind="ExternalOutput").ap())
    xattn_ffn_kernel(nc, *args)
    r = _run(nc, [arrays], core_ids=[0])
    return r.results[0]["out_0_dram"]
```

```python
import math
from contextlib import ExitStack

import numpy as np

import concourse.bass as bass
from concourse import mybir

P = 128
ALU = mybir.AluOpType
ACT = mybir.ActivationFunctionType
F32 = mybir.dt.float32
BF16 = mybir.dt.bfloat16
I32 = mybir.dt.int32
U32 = mybir.dt.uint32
AX_X = mybir.AxisListType.X
MAGIC = 1.5 * 2.0 ** 23
EPS = 1e-5


class Turn:

    def __init__(self, i, c, u=2):
        self.i, self.c, self.u = i, c, u

    def plus(self, d):
        return Turn(self.i, self.c + d, self.u)

    def times(self, m, d=0):
        return self.i * (self.u * m) + (self.c * m + d)

    @property
    def n(self):
        return self.times(1)

    def slot(self, ring):
        return self.c % ring

    def round(self, ring):
        return self.i * (self.u // ring) + self.c // ring

    @property
    def par(self):
        return self.slot(2)

    @property
    def half(self):
        return self.round(2)

    def within(self, end):
        return not isinstance(self.i, int) or 0 <= self.n < end


def xattn_ffn_kernel(nc, x, ctx_in, pos, Wq, Wkv, Wout, bout, Wg, W1, W2, W3, out):
    B, N, D = x.shape
    CD = ctx_in.shape[2]
    E, H, _ = W1.shape
    TOKENS = B * N
    T = TOKENS // P
    KC = D // P
    HEADS, HD = 32, 8
    GH = 8
    G = HEADS // GH
    GW = GH * HD
    SCALE = float(np.float32(1.0) / np.sqrt(np.float32(HD)))
    HA = 96
    HB = H - HA
    OVER = HA - HB
    RC = TOKENS + P
    NBLK = 2 * TOKENS // P + E - 1
    SPARE = E - 1
    RW = D + 1
    NOWHERE = 1 << 20
    assert N == 64 and P == 2 * N and T % 8 == 0 and NBLK % 4 == 3 and CD == P and D == 2 * P

    x_rows = x.rearrange("b n d -> (b n) d")
    ctx_rows = ctx_in.rearrange("b n d -> (b n) d")
    out_rows = out.rearrange("b n d -> (b n) d")
    pos_rows = pos.rearrange("b n c -> (b n) c").rearrange("(t p) c -> p t c", p=P)
    routed = nc.dram_tensor("routed_rows", (E * RC + SPARE * P, RW), F32, kind="Internal").ap()
    results = nc.dram_tensor("result_rows", (2 * TOKENS, D), F32, kind="Internal").ap()

    with ExitStack() as es:
        def sb(name, shape, dt=F32):
            return es.enter_context(nc.sbuf_tensor(name, shape, dt))

        def sem(name):
            return es.enter_context(nc.semaphore(name))

        banks = [es.enter_context(nc.psum_tensor(f"bank{n}", [P, 512], F32)) for n in range(8)]
        ps_l, ps_pt, ps_qk, ps_vo, ps_nd, ps_tr = banks[0:2], banks[2:4], banks[4], banks[5], banks[6], banks[7]

        xres = sb("xres", [P, T, D])
        x_sb = sb("x_sb", [P, 2, D])
        ctx_sb = sb("ctx_sb", [P, 2, CD])
        xn = sb("xn", [P, 2, D])
        stats = sb("stats", [P, 2, 6])
        mv1 = sb("mv1", [P, 2, 2])
        rstd1 = sb("rstd1", [P, 2])
        mv2 = sb("mv2", [P, 2, 2])
        rstd2 = sb("rstd2", [P, 2])
        var_eps1 = sb("var_eps1", [P, 1])
        var_eps2 = sb("var_eps2", [P, 1])
        minus_half = sb("minus_half", [P, 1])
        xT = sb("xT", [P, 2, 3 * P])
        rope_a = sb("rope_a", [P, 512])
        rope_b = sb("rope_b", [P, 512])
        rot = sb("rot", [P, 512])
        kT = sb("kT", [P, 2, G, N])
        qbd = sb("qbd", [P, 2, G, P])
        km = sb("km", [P, 2, G, GH, N])
        vst = sb("vst", [P, 2, 2 * HEADS // 2, 32])
        rowmax = sb("rowmax", [P, 2, GH])
        shifted = sb("shifted", [P, 2, 512])
        expd = sb("expd", [P, 2, 512])
        pT = sb("pT", [P, G, 512])
        rden = sb("rden", [P, D])
        attnT = sb("attnT", [P, D])
        xs = sb("xs", [P, 2, 2, RW])
        x2T = sb("x2T", [P, D])
        top8 = sb("top8", [P, 8])
        idx8 = sb("idx8", [P, 8], U32)
        onehot = sb("onehot", [P, 2, E])
        chosen = sb("chosen", [P, E], BF16)
        seen = sb("seen", [P, E], BF16)
        place = sb("place", [P, E])
        place2 = sb("place2", [P, 2, E])
        slots = sb("slots", [P, 2, 2], I32)
        topv = sb("topv", [P, T, 2])
        ident = sb("ident", [P, P])
        tri = sb("tri", [P, P], BF16)
        ones_bf = sb("ones_bf", [P, P], BF16)
        mask32 = sb("mask32", [P, 32])
        mask = sb("mask", [P, GH])
        ones_pair = sb("ones_pair", [P, 2, 32])
        bout_sb = sb("bout_sb", [P, D])
        pos_sb = sb("pos_sb", [P, T, 2])
        ang = sb("ang", [P, 2, T, 2, 2])
        turns = sb("turns", [P, 2 * T * 4])
        cos_t = sb("cos_t", [P, T, 4])
        sin_t = sb("sin_t", [P, T, 2, 4])
        iota_e = sb("iota_e", [P, E])
        iota_ei = sb("iota_ei", [P, E], I32)
        region = sb("region", [P, E])
        dest_i = sb("dest_i", [P, T, 2], I32)
        dest = sb("dest", [P, T, 2])
        pad_row = sb("pad_row", [P, RW])
        wq_raw = sb("wq_raw", [P, KC, D])
        wkv_raw = sb("wkv_raw", [P, 2 * D])
        wq_p = sb("wq_p", [P, KC, D])
        wk_p = sb("wk_p", [P, D])
        wv_p = sb("wv_p", [P, 2, P])
        wout_sb = sb("wout_sb", [P, KC, D])
        wg_raw = sb("wg_raw", [E, D])
        wgT = sb("wgT", [P, KC, E])
        w1a = sb("w1a", [P, E, D])
        w1b = sb("w1b", [H - P, E, D])
        w12T = sb("w12T", [P, E, KC, 2 * H])
        w3_raw = sb("w3_raw", [P, KC, E, H])
        w3T = sb("w3T", [HA, E, 2, D])
        cntf = sb("cntf", [1, E])
        nblk = sb("nblk", [1, E])
        nblk2 = sb("nblk2", [1, E])
        skip = sb("skip", [1, E])
        blk_end = sb("blk_end", [1, E])
        onesrow = sb("onesrow", [1, E])
        jrow_i = sb("jrow_i", [1, NBLK], I32)
        jrow = sb("jrow", [1, NBLK])
        ended = sb("ended", [1, NBLK, E])
        ended_n = sb("ended_n", [1, NBLK, E])
        blk_exp = sb("blk_exp", [1, NBLK])
        blk_first = sb("blk_first", [1, NBLK])
        blk_row = sb("blk_row", [1, NBLK])
        cnt_i = sb("cnt_i", [1, E], I32)
        exp_i = sb("exp_i", [1, NBLK], I32)
        row_i = sb("row_i", [1, NBLK], I32)
        RB = 4
        xb = sb("xb", [P, RB, RW])
        xbT = sb("xbT", [P, 2, D])
        act_h = sb("act_h", [P, 2, H])
        gated = sb("gated", [P, 2, H])
        blk_dest = sb("blk_dest", [P, RB], I32)
        wdiff = sb("wdiff", [P, T])
        wexp = sb("wexp", [P, T])
        wsum = sb("wsum", [P, T])
        wtop = sb("wtop", [P, 2, T])

        wqk_in = sem("wqk_in")
        wqk_ready = sem("wqk_ready")
        pos_in = sem("pos_in")
        w_in = sem("w_in")
        wf1_in = sem("wf1_in")
        wf2_in = sem("wf2_in")
        wf3_in = sem("wf3_in")
        in_tile = [sem("in_even"), sem("in_odd")]
        pool_const = sem("pool_const")
        pool_step = sem("pool_step")
        dve_const = sem("dve_const")
        dve_step = sem("dve_step")
        rope_tables = sem("rope_tables")
        wt_done = sem("wt_done")
        waits_over = sem("waits_over")
        wt_sb = [sem("wt_sb_even"), sem("wt_sb_odd")]
        stats1_done, mv1_done, rstd1_done, xn_done, xb_done = (
            sem(s) for s in ("stats1_done", "mv1_done", "rstd1_done", "xn_done", "xb_done"))
        eps1_done, eps2_done = sem("eps1_done"), sem("eps2_done")
        xT_done, xT_sb, qk_done, v_done, v_sb = (sem(s) for s in ("xT_done", "xT_sb", "qk_done", "v_done", "v_sb"))
        rope_done, rot_done = sem("rope_done"), sem("rot_done")
        kqT_done, kT_sb, qT_sb, km_done = (sem(s) for s in ("kqT_done", "kT_sb", "qT_sb", "km_done"))
        l_done, max_done, shift_done, exp_done, pt_done, pt_sb, pv_done = (
            sem(s) for s in ("l_done", "max_done", "shift_done", "exp_done", "pt_done", "pt_sb", "pv_done"))
        rden_done, norm_done, out_done, x1_done = (sem(s) for s in ("rden_done", "norm_done", "out_done", "x1_done"))
        stats2_done, mv2_done, rstd2_done, x2n_done = (
            sem(s) for s in ("stats2_done", "mv2_done", "rstd2_done", "x2n_done"))
        x2c_done = sem("x2c_done")
        x2T_done, x2T_sb, gate_done, top_done, rank_done, rank_read, slot_done = (
            sem(s) for s in ("x2T_done", "x2T_sb", "gate_done", "top_done", "rank_done", "rank_read", "slot_done"))
        route_step = sem("route_step")
        chosen_done = sem("chosen_done")
        scattered = [sem("scattered_even"), sem("scattered_odd")]
        spare_in = sem("spare_in")
        cnt_done, cnt_i_done, tab_step, row_done, pad_in, pad2_in = (
            sem(s) for s in ("cnt_done", "cnt_i_done", "tab_step", "row_done", "pad_in", "pad2_in"))
        blk_in = [sem(f"blk_in{n}") for n in range(RB)]
        bT_done, bT_sb, h_done, silu_done, gated_done, hT_done, hT_sb, y_done, y_copied = (
            sem(s) for s in ("bT_done", "bT_sb", "h_done", "silu_done", "gated_done", "hT_done", "hT_sb",
                             "y_done", "y_copied"))
        y_out = [sem(f"y_out{n}") for n in range(RB)]
        dest_done = sem("dest_done")
        wdiff_done, wexp_done, wtop_done = sem("wdiff_done"), sem("wexp_done"), sem("wtop_done")
        wg_done, wg_sb, w3_zero = sem("wg_done"), sem("wg_sb"), sem("w3_zero")
        y_back = [sem(f"y_back{n}") for n in range(4)]
        half_done, o_done = sem("half_done"), sem("o_done")
        o_stored = [sem(f"o_stored{n}") for n in range(4)]

        N_POOL_CONST, N_DVE_CONST, N_W = 9, 9, 3
        NWT = E * KC * 2 + E
        wt_banks = [banks[0], banks[1], banks[2], banks[3]]
        ps_h, ps_y, ps_hT = banks[0:2], banks[2:4], banks[4:6]
        w2a = km[:, 0].rearrange("p g h k -> p (g h k)").rearrange("p (e d) -> p e d", e=E)
        w2b = km[0:H - P, 1].rearrange("p g h k -> p (g h k)").rearrange("p (e d) -> p e d", e=E)
        y_in = km[:].rearrange("p u g (b h) k -> p (u g) (b h k)", b=2).rearrange(
            "p (v k) (a d) -> p v k a d", k=2, d=D)
        o_sb = pT[:].rearrange("p v (a d) -> p v a d", a=2)
        y_half = rope_a[:].rearrange("p (a d) -> p a d", a=2)
        y_sb = shifted[:].rearrange("p a (b d) -> p (a b) d", b=2)
        hT = rope_b[0:HA].rearrange("p (a c t) -> p a c t", a=2, c=2)

        def weight_bank(n):
            if n < E * KC:
                return 1, n // KC, n % KC
            if n < E * KC + E:
                return 3, n - E * KC, 0
            n -= E * KC + E
            return 2, n // KC, n % KC

        def weight_copy(n):
            kind, e, c = weight_bank(n)
            ps = wt_banks[n % 4]
            if kind == 3:
                return w3T[:, e].rearrange("p c d -> p (c d)"), ps[0:HA, 0:2 * D]
            first = 0 if kind == 1 else H
            return w12T[:, e, c, first:first + H], ps[:, 0:H]

        def is_first(t, ahead):
            return isinstance(t.i, int) and t.c == -ahead

        def banks_of(t, slot):
            if not isinstance(t.i, int) or t.c < T:
                return range(0)
            k = (t.c - T) * 4 + slot
            return range(k * NWT // 12, (k + 1) * NWT // 12)

        block = es.enter_context(nc.Block())

        def apart(eng):
            eng.sem_inc(waits_over, 1)

        def wait_past(eng, semaphore, value):
            if not (isinstance(value, int) and value <= 0):
                eng.wait_ge(semaphore, value)

        def pipeline(eng, body):
            def do(stage, t, *args):
                if t.within(T):
                    stage(t, *args)
            for c in range(-4, 5):
                body(do, Turn(0, c))
            with eng.Fori(2, (T - 6) // 2) as i:
                body(do, Turn(i, 1))
                body(do, Turn(i, 2))
            for c in range(T - 5, T + 3):
                body(do, Turn(0, c))

        def blocks(eng, body, before, after, prepare=None):
            def do(stage, b):
                if b.within(NBLK):
                    stage(b)
            for c in range(-before, 7):
                body(do, Turn(0, c, 4))
            with eng.Fori(1, (NBLK - 7) // 4) as i:
                if prepare:
                    prepare(i)
                for c in range(3, 7):
                    body(do, Turn(i, c, 4))
            for c in range(NBLK - 4, NBLK + after):
                body(do, Turn(0, c, 4))

        def pad_experts(eng, first, padded):
            eng.wait_ge(cnt_i_done, 1)
            counts = [eng.alloc_register(f"count{first + n}") for n in range(E // 2)]
            eng.load(counts, cnt_i[0:1, first:first + E // 2])
            for n, reg in enumerate(counts):
                rows = eng.snap(reg, min_val=0, max_val=TOKENS)
                eng.dma_start(routed[bass.ds(rows + (first + n) * RC, P), :], pad_row[:]).then_inc(padded, 16)

        def upto(value):
            return min(value, T) if isinstance(value, int) else value

        @block.sync
        def _(sp):
            def load_tile(t):
                wait_past(sp, xb_done, t.n - 1)
                apart(sp)
                wait_past(sp, xT_done, t.n - 1)
                apart(sp)
                sp.dma_start(x_sb[:, t.par, :], x_rows[bass.ds(t.times(P), P), :]).then_inc(in_tile[t.par], 16)
                sp.dma_start(ctx_sb[:, t.par, :], ctx_rows[bass.ds(t.times(P), P), :]).then_inc(in_tile[t.par], 16)

            load_tile(Turn(0, 0))
            sp.dma_start(wkv_raw[:], Wkv).then_inc(wqk_in, 16)
            sp.dma_start(wq_raw[:], Wq.rearrange("(c p) n -> p c n", p=P)).then_inc(wqk_in, 16)
            sp.dma_start(pos_sb[:], pos_rows).then_inc(pos_in, 16)
            load_tile(Turn(0, 1))
            sp.dma_start(wg_raw[:], Wg).then_inc(w_in, 16)
            sp.dma_start(bout_sb[:], bout.rearrange("(a n) -> a n", a=1).broadcast_to([P, D])).then_inc(w_in, 16)
            sp.dma_start(wout_sb[:], Wout.rearrange("(c p) n -> p c n", p=P)).then_inc(w_in, 16)
            load_tile(Turn(0, 2))
            load_tile(Turn(0, 3))
            sp.dma_start(w1a[:], W1[:, 0:P, :].rearrange("e h d -> h e d")).then_inc(wf1_in, 16)
            sp.dma_start(w1b[:], W1[:, P:H, :].rearrange("e h d -> h e d")).then_inc(wf1_in, 16)
            for c in range(KC):
                sp.dma_start(w3_raw[:, c], W3[:, c * P:(c + 1) * P, :].rearrange("e p h -> p e h")).then_inc(wf3_in, 16)
            sp.wait_ge(pool_const, N_POOL_CONST)
            for s in range(SPARE):
                r0 = E * RC + s * P
                sp.dma_start(routed[r0:r0 + P, :], pad_row[:]).then_inc(spare_in, 16)
            with sp.Fori(2, T // 2) as i:
                load_tile(Turn(i, 0))
                load_tile(Turn(i, 1))

            sp.wait_ge(l_done, T * G)
            sp.dma_start(w2a, W2[:, 0:P, :].rearrange("e h d -> h e d")).then_inc(wf2_in, 16)
            sp.dma_start(w2b, W2[:, P:H, :].rearrange("e h d -> h e d")).then_inc(wf2_in, 16)
            pad_experts(sp, 0, pad_in)
            sp.wait_ge(row_done, 1)
            sp.wait_ge(pad_in, 16 * (E // 2))
            sp.wait_ge(pad2_in, 16 * (E // 2))
            sp.wait_ge(spare_in, 16 * SPARE)
            for par in range(2):
                sp.wait_ge(scattered[par], 32 * (T // 2))

            def load_block(b):
                wait_past(sp, bT_done, b.n - RB + 1)
                apart(sp)
                wait_past(sp, dest_done, b.n - RB + 1)
                apart(sp)
                row = sp.value_load(row_i[0:1, bass.ds(b.n, 1)], min_val=0, max_val=E * RC + (SPARE - 1) * P)
                sp.dma_start(xb[:, b.slot(RB), :], routed[bass.ds(row, P), :]).then_inc(blk_in[b.slot(RB)], 16)

            blocks(sp, lambda do, b: do(load_block, b), 0, 0)

            for n in range(RB):
                sp.wait_ge(y_out[n], 16 * ((NBLK - n + RB - 1) // RB))
            back = results.rearrange("(k r) d -> k r d", k=2)

            def load_results(i, u):
                for k in range(2):
                    r0 = i * (8 * P) + u * 2 * P
                    sp.dma_start(y_in[:, u, k], back[k, bass.ds(r0, 2 * P), :].rearrange("(a p) d -> p a d", p=P))\
                        .then_inc(y_back[u], 16)

            for u in range(4):
                load_results(0, u)
            with sp.Fori(1, T // 8) as i:
                for u in range(4):
                    sp.wait_ge(o_done, i * 8 + (2 * u - 6))
                    apart(sp)
                    load_results(i, u)

        @block.gpsimd
        def _(pool):
            nc.gpsimd.memset(minus_half[:], -0.5).then_inc(pool_const, 1)
            nc.gpsimd.memset(ident[:], 0.0).then_inc(pool_step, 1)
            nc.gpsimd.memset(mask32[:], 1.0).then_inc(pool_step, 1)
            nc.gpsimd.memset(tri[:], 1.0).then_inc(pool_step, 1)
            nc.gpsimd.memset(pad_row[:], 0.0).then_inc(pool_step, 1)
            pool.wait_ge(pool_step, 4)
            nc.gpsimd.affine_select(out=ident[:], in_=ident[:], compare_op=ALU.not_equal, fill=1.0, base=0,
                                    pattern=[[-1, P]], channel_multiplier=1).then_inc(pool_const, 1)
            nc.gpsimd.affine_select(out=mask32[:], in_=mask32[:], compare_op=ALU.is_ge, fill=0.0, base=0,
                                    pattern=[[-4, 32]], channel_multiplier=1).then_inc(pool_step, 1)
            pool.wait_ge(pool_step, 5)
            nc.gpsimd.affine_select(out=mask32[:], in_=mask32[:], compare_op=ALU.is_ge, fill=0.0, base=3,
                                    pattern=[[4, 32]], channel_multiplier=-1).then_inc(pool_const, 1)
            nc.gpsimd.affine_select(out=tri[:], in_=tri[:], compare_op=ALU.is_gt, fill=0.0, base=0,
                                    pattern=[[1, P]], channel_multiplier=-1).then_inc(pool_const, 1)
            nc.gpsimd.iota(dest_i[:], [[P, T], [TOKENS, 2]], base=0, channel_multiplier=1).then_inc(pool_const, 1)
            nc.gpsimd.iota(iota_ei[:], [[1, E]], base=0, channel_multiplier=0).then_inc(pool_const, 1)
            nc.gpsimd.iota(jrow_i[:], [[1, NBLK]], base=0, channel_multiplier=0).then_inc(pool_const, 1)
            nc.gpsimd.memset(pad_row[:, D:RW], float(NOWHERE)).then_inc(pool_const, 1)
            nc.gpsimd.memset(onesrow[:], 1.0).then_inc(pool_const, 1)

            def rstd_of_x(t):
                pool.wait_ge(mv1_done, t.n + 1)
                wait_past(pool, rstd1_done, t.n)
                apart(pool)
                nc.gpsimd.tensor_scalar(var_eps1[:], mv1[:, t.par, 1:2], EPS, None, ALU.add).then_inc(eps1_done, 1)
                pool.wait_ge(eps1_done, t.n + 1)
                wait_past(pool, xn_done, t.n - 1)
                nc.gpsimd.tensor_tensor(rstd1[:, t.par:t.par + 1], var_eps1[:], minus_half[:], ALU.pow)\
                    .then_inc(rstd1_done, 1)

            def rstd_of_x1(t):
                pool.wait_ge(mv2_done, t.n + 1)
                wait_past(pool, rstd2_done, t.n)
                apart(pool)
                nc.gpsimd.tensor_scalar(var_eps2[:], mv2[:, t.par, 1:2], EPS, None, ALU.add).then_inc(eps2_done, 1)
                pool.wait_ge(eps2_done, t.n + 1)
                wait_past(pool, x2n_done, t.times(2))
                nc.gpsimd.tensor_tensor(rstd2[:, t.par:t.par + 1], var_eps2[:], minus_half[:], ALU.pow)\
                    .then_inc(rstd2_done, 1)

            def normalise_x(t):
                pool.wait_ge(rstd1_done, t.n + 1)
                wait_past(pool, xT_done, t.n - 1)
                apart(pool)
                nc.gpsimd.tensor_scalar(xn[:, t.par, :], x_sb[:, t.par, :], mv1[:, t.par, 0:1],
                                        rstd1[:, t.par:t.par + 1], ALU.subtract, ALU.mult).then_inc(xn_done, 1)

            def add_bias(t):
                pool.wait_ge(w_in, 16 * N_W)
                nc.gpsimd.tensor_tensor(xres[:, bass.ds(t.n, 1), :].rearrange("p a d -> p (a d)"),
                                        x_sb[:, t.par, :], bout_sb[:], ALU.add).then_inc(xb_done, 1)

            def rotate(t):
                pool.wait_ge(rope_done, t.n + 1)
                wait_past(pool, kqT_done, t.n)
                nc.gpsimd.tensor_tensor(rot[:], rope_a[:], rope_b[:], ALU.add).then_inc(rot_done, 1)

            def mask_keys(t, first):
                pool.wait_ge(kT_sb, t.n + 1)
                wait_past(pool, l_done, t.times(G, -G))
                for g in range(first, first + 2):
                    nc.gpsimd.tensor_tensor(km[:, t.par, g], kT[:, t.par, g].unsqueeze(1).broadcast_to([P, GH, N]),
                                            mask[:].unsqueeze(2).broadcast_to([P, GH, N]), ALU.mult)\
                        .then_inc(km_done, 1)

            def scatter(t):
                pool.wait_ge(slot_done, t.n + 1)
                pool.wait_ge(x2c_done, t.n + 1)
                apart(pool)
                for k in range(2):
                    nc.gpsimd.indirect_dma_start(
                        routed[:, :], bass.IndirectOffsetOnAxis(ap=slots[:, t.par, k:k + 1], axis=0),
                        xs[:, t.par, k, :], None).then_inc(scattered[t.par], 16)

            pool.wait_ge(dve_const, N_DVE_CONST)

            def body(do, t):
                do(mask_keys, t.plus(1), 0)
                do(rstd_of_x1, t.plus(-2))
                do(mask_keys, t.plus(1), 2)
                do(rotate, t.plus(2))
                do(rstd_of_x, t.plus(4))
                do(normalise_x, t.plus(4))
                do(add_bias, t.plus(4))
                do(scatter, t.plus(-3))

            pipeline(pool, body)

            def take_dest(b):
                pool.wait_ge(blk_in[b.slot(RB)], b.round(RB) * 16 + 16)
                wait_past(pool, y_out[b.slot(RB)], b.round(RB) * 16)
                apart(pool)
                nc.gpsimd.tensor_copy(blk_dest[:, b.slot(RB):b.slot(RB) + 1], xb[:, b.slot(RB), D:RW])\
                    .then_inc(dest_done, 1)

            def store_block(b):
                pool.wait_ge(y_copied, b.n + 1)
                pool.wait_ge(dest_done, b.n + 1)
                apart(pool)
                nc.gpsimd.indirect_dma_start(
                    results[:, :], bass.IndirectOffsetOnAxis(ap=blk_dest[:, b.slot(RB):b.slot(RB) + 1], axis=0),
                    y_sb[:, b.slot(RB), :], None, bounds_check=2 * TOKENS - 1, oob_is_err=False)\
                    .then_inc(y_out[b.slot(RB)], 16)

            pool.wait_ge(wt_sb[0], NWT // 2)
            pool.wait_ge(wt_sb[1], NWT // 2)
            nc.gpsimd.memset(w3T[0:OVER, :, 1, :], 0.0).then_inc(w3_zero, 1)

            def ffn_body(do, b):
                do(take_dest, b)
                do(store_block, b.plus(-2))

            blocks(pool, ffn_body, 0, 2)

        @block.vector
        def _(dve):
            V = nc.vector

            def stats_of_x(t):
                dve.wait_ge(in_tile[t.par], t.half * 32 + 32)
                wait_past(dve, mv1_done, t.n)
                apart(dve)
                V.bn_stats(stats[:, 0, :], x_sb[:, t.par, :]).then_inc(stats1_done, 1)

            def mean_of_x(t):
                dve.wait_ge(stats1_done, t.n + 1)
                wait_past(dve, xn_done, t.n - 1)
                apart(dve)
                V.bn_aggr(mv1[:, t.par, :], stats[:, 0, :]).then_inc(mv1_done, 1)

            def rope(t):
                dve.wait_ge(qk_done, t.n + 1)
                if is_first(t, 0):
                    dve.wait_ge(rope_tables, 4)
                wait_past(dve, rot_done, t.n)
                cos = cos_t[:, bass.ds(t.n, 1), :].rearrange("p a c -> p (a c)")
                V.tensor_tensor(rope_a[:].rearrange("p (s c) -> p s c", c=4),
                                ps_qk[:].rearrange("p (s c) -> p s c", c=4),
                                cos.unsqueeze(1).broadcast_to([P, P, 4]), ALU.mult)
                for i in range(2):
                    sn = sin_t[:, bass.ds(t.n, 1), i, :].rearrange("p a c -> p (a c)")
                    o = rope_b[:].rearrange("p (s i h c) -> p s i h c", s=2 * G, i=2, c=4)[:, :, i]
                    q = ps_qk[:].rearrange("p (s i h c) -> p s i h c", s=2 * G, i=2, c=4)[:, :, 1 - i]
                    ins = V.tensor_tensor(o, q, sn.unsqueeze(1).unsqueeze(1).broadcast_to([P, 2 * G, GH, 4]), ALU.mult)
                ins.then_inc(rope_done, 1)

            def grouped_logits(g):
                return ps_l[g % 2][:].rearrange("p (h k) -> p h k", k=N)

            def peak(t, g):
                dve.wait_ge(l_done, t.times(G, g + 1))
                wait_past(dve, shift_done, t.times(G, g - 1))
                V.tensor_reduce(rowmax[:, g % 2, :], grouped_logits(g), AX_X, ALU.max).then_inc(max_done, 1)

            def shift(t, g):
                dve.wait_ge(max_done, t.times(G, g + 1))
                wait_past(dve, exp_done, t.times(G, g - 1))
                V.tensor_tensor(shifted[:, g % 2, :].rearrange("p (h k) -> p h k", k=N), grouped_logits(g),
                                rowmax[:, g % 2, :].unsqueeze(2).broadcast_to([P, GH, N]), ALU.subtract)\
                    .then_inc(shift_done, 1)

            def invert_sums(t):
                dve.wait_ge(pv_done, t.times(2, 2))
                wait_past(dve, norm_done, t.n)
                V.reciprocal(rden[:], ps_nd[:, D:2 * D]).then_inc(rden_done, 1)

            def normalise_attn(t):
                dve.wait_ge(rden_done, t.n + 1)
                wait_past(dve, out_done, t.n)
                V.tensor_tensor(attnT[:], ps_nd[:, 0:D], rden[:], ALU.mult).then_inc(norm_done, 1)

            def row(t):
                return xres[:, bass.ds(t.n, 1), :].rearrange("p a d -> p (a d)")

            def residual(t):
                dve.wait_ge(out_done, t.n + 1)
                dve.wait_ge(xb_done, t.n + 1)
                V.tensor_tensor(row(t), ps_vo[:, 0:D], row(t), ALU.add).then_inc(x1_done, 1)

            def stats_of_x1(t):
                dve.wait_ge(x1_done, t.n + 1)
                wait_past(dve, mv2_done, t.n)
                apart(dve)
                V.bn_stats(stats[:, 1, :], row(t)).then_inc(stats2_done, 1)

            def mean_of_x1(t):
                dve.wait_ge(stats2_done, t.n + 1)
                wait_past(dve, x2n_done, t.times(2))
                apart(dve)
                V.bn_aggr(mv2[:, t.par, :], stats[:, 1, :]).then_inc(mv2_done, 1)

            def normalise_x1(t):
                dve.wait_ge(rstd2_done, t.n + 1)
                wait_past(dve, scattered[t.par], t.half * 32)
                wait_past(dve, x2T_done, t.n)
                V.tensor_scalar(xs[:, t.par, 0, 0:D], row(t), mv2[:, t.par, 0:1], rstd2[:, t.par:t.par + 1],
                                ALU.subtract, ALU.mult).then_inc(x2n_done, 1)
                V.tensor_copy(xs[:, t.par, :, D:RW],
                              dest[:, bass.ds(t.n, 1), :].rearrange("p a k -> p (a k)").unsqueeze(2))\
                    .then_inc(x2n_done, 1)

            def best_scores(t):
                dve.wait_ge(gate_done, t.n + 1)
                wait_past(dve, slot_done, t.n)
                apart(dve)
                V.max(top8[:], ps_vo[:, 0:E]).then_inc(route_step, 1)

            def best_experts(t):
                dve.wait_ge(route_step, t.times(4, 1))
                apart(dve)
                V.max_index(idx8[:], top8[:], ps_vo[:, 0:E]).then_inc(route_step, 1)
                V.tensor_copy(topv[:, bass.ds(t.n, 1), :].rearrange("p a k -> p (a k)"), top8[:, 0:2])

            def mark_choices(t):
                dve.wait_ge(route_step, t.times(4, 2))
                V.tensor_tensor(onehot[:], iota_e[:].unsqueeze(1).broadcast_to([P, 2, E]),
                                idx8[:, 0:2].unsqueeze(2).broadcast_to([P, 2, E]), ALU.is_equal).then_inc(route_step, 1)

            def join_choices(t):
                dve.wait_ge(route_step, t.times(4, 3))
                wait_past(dve, rank_done, t.n)
                V.tensor_tensor(chosen[:], onehot[:, 0, :], onehot[:, 1, :], ALU.add).then_inc(top_done, 1)

            def place_tokens(t):
                dve.wait_ge(rank_done, t.n + 1)
                wait_past(dve, chosen_done, t.n)
                V.tensor_tensor(place[:], ps_vo[:, E:2 * E], region[:], ALU.add).then_inc(rank_read, 1)
                V.tensor_tensor(seen[:], seen[:], chosen[:], ALU.add).then_inc(chosen_done, 1)

            def select_places(t):
                dve.wait_ge(rank_read, t.n + 1)
                V.tensor_tensor(place2[:], onehot[:], place[:].unsqueeze(1).broadcast_to([P, 2, E]), ALU.mult)\
                    .then_inc(route_step, 1)

            def set_slots(t):
                dve.wait_ge(route_step, t.times(4, 4))
                with nc.allow_low_precision(reason="sums of one row number and zeros"):
                    V.tensor_reduce(slots[:, t.par, :], place2[:], AX_X, ALU.add).then_inc(slot_done, 1)

            steps = [0]

            def step(ins):
                steps[0] += 1
                ins.then_inc(dve_step, 1)
                dve.wait_ge(dve_step, steps[0])

            V.memset(qbd[:], 0.0).then_inc(dve_const, 1)
            V.memset(vst[:], 0.0).then_inc(dve_const, 1)
            V.memset(seen[:], 0.0).then_inc(dve_const, 1)
            V.memset(ones_bf[:], 1.0).then_inc(dve_const, 1)
            step(V.memset(ones_pair[:], 0.0))
            for par in range(2):
                for h in range(2):
                    ins = V.memset(ones_pair[64 * h:64 * h + 64, par, 16 * par + 8 * h:16 * par + 8 * h + 8], 1.0)
            ins.then_inc(dve_const, 1)
            dve.wait_ge(pool_const, N_POOL_CONST)
            V.tensor_reduce(mask[:], mask32[:].rearrange("p (a h) -> p h a", h=GH), AX_X, ALU.add)\
                .then_inc(dve_const, 1)
            step(V.tensor_copy(iota_e[:], iota_ei[:]))
            V.tensor_scalar(region[:], iota_e[:], float(RC), None, ALU.mult).then_inc(dve_const, 1)
            V.tensor_copy(jrow[:], jrow_i[:]).then_inc(dve_const, 1)
            V.tensor_copy(dest[:], dest_i[:]).then_inc(dve_const, 1)

            def prepare():
                dve.wait_ge(wqk_in, 32)
                for c in range(KC):
                    V.tensor_copy(wq_p[:, c].rearrange("p (g i m) -> p g i m", g=G, i=2),
                                  wq_raw[:, c].rearrange("p (g m i) -> p g i m", g=G, i=2)).then_inc(wqk_ready, 1)
                V.tensor_copy(wk_p[:].rearrange("p (g i m) -> p g i m", g=G, i=2),
                              wkv_raw[:, 0:D].rearrange("p (g m i) -> p g i m", g=G, i=2)).then_inc(wqk_ready, 1)
                V.tensor_copy(wv_p[:].rearrange("p o (h d) -> p o h d", d=HD),
                              wkv_raw[:, D:2 * D].rearrange("p (h o d) -> p o h d", o=2, d=HD)).then_inc(wqk_ready, 1)
                dve.wait_ge(pos_in, 16)
                step(V.tensor_copy(ang[:, 0, :, :, 0], pos_sb[:]))
                step(V.tensor_scalar(ang[:, 0, :, :, 1], pos_sb[:], 10000.0 ** -0.5, None, ALU.mult))
                step(V.tensor_scalar(ang[:, 1], ang[:, 0], math.pi / 2, None, ALU.add))
                af = ang[:].rearrange("p a t c h -> p (a t c h)")
                step(V.tensor_scalar(turns[:], af, 1 / (2 * math.pi), MAGIC, ALU.mult, ALU.add))
                step(V.tensor_scalar(turns[:], turns[:], MAGIC, None, ALU.subtract))
                step(V.scalar_tensor_tensor(af, turns[:], -6.28125, af, ALU.mult, ALU.add))
                step(V.scalar_tensor_tensor(af, turns[:], -(2 * math.pi - 6.28125), af, ALU.mult, ALU.add))
                V.tensor_scalar(af, af, 3.1415925, -3.1415925, ALU.min, ALU.max).then_inc(rope_tables, 1)

            def weights(t, slot):
                for n in banks_of(t, slot):
                    if n % 2 == 1:
                        dve.wait_ge(wt_done, n + 1)
                        into, ps = weight_copy(n)
                        V.tensor_copy(into, ps).then_inc(wt_sb[1], 1)

            def body(do, t):
                do(peak, t, 1)
                do(residual, t.plus(-2))
                do(shift, t, 1)
                do(stats_of_x1, t.plus(-2))
                do(rope, t.plus(2))
                do(mean_of_x1, t.plus(-2))
                weights(t, 0)

                do(peak, t, 2)
                do(shift, t, 2)
                do(invert_sums, t.plus(-1))
                do(normalise_x1, t.plus(-2))
                do(normalise_attn, t.plus(-1))
                weights(t, 1)

                do(peak, t, 3)
                do(shift, t, 3)
                do(best_scores, t.plus(-3))
                do(stats_of_x, t.plus(4))
                do(best_experts, t.plus(-3))
                do(mean_of_x, t.plus(4))
                if is_first(t, 4):
                    prepare()
                do(mark_choices, t.plus(-3))
                weights(t, 2)

                do(peak, t.plus(1), 0)
                do(join_choices, t.plus(-3))
                do(shift, t.plus(1), 0)
                do(place_tokens, t.plus(-3))
                do(select_places, t.plus(-3))
                do(set_slots, t.plus(-3))
                weights(t, 3)

            pipeline(dve, body)

            dve.wait_ge(cnt_done, 1)
            tabs = [0]

            def tab(ins):
                tabs[0] += 1
                ins.then_inc(tab_step, 1)
                dve.wait_ge(tab_step, tabs[0])

            tab(V.tensor_copy(cntf[:], ps_vo[0:1, 0:E]))
            V.tensor_copy(cnt_i[:], cntf[:]).then_inc(cnt_i_done, 1)
            tab(V.tensor_scalar(nblk[:], cntf[:], 1.0 / P, (P - 1) / P - 0.5 + 0.5 / P, ALU.mult, ALU.add))
            tab(V.tensor_scalar(nblk[:], nblk[:], MAGIC, None, ALU.add))
            tab(V.tensor_scalar(nblk2[:], nblk[:], MAGIC, None, ALU.subtract))
            V.tensor_scalar(skip[:], nblk2[:], -float(P), float(RC), ALU.mult, ALU.add)
            tab(V.tensor_tensor_scan(blk_end[:], onesrow[:], nblk2[:], 0.0, ALU.mult, ALU.add))
            je = [1, NBLK, E]
            tab(V.tensor_tensor(ended[:], jrow[:].unsqueeze(2).broadcast_to(je),
                                blk_end[:].unsqueeze(1).broadcast_to(je), ALU.is_ge))
            tab(V.tensor_tensor(ended_n[:], ended[:], skip[:].unsqueeze(1).broadcast_to(je), ALU.mult))
            tab(V.tensor_reduce(blk_first[:], ended_n[:], AX_X, ALU.add))
            tab(V.scalar_tensor_tensor(blk_row[:], jrow[:], float(P), blk_first[:], ALU.mult, ALU.add))
            V.tensor_copy(row_i[:], blk_row[:]).then_inc(row_done, 1)
            tab(V.tensor_reduce(blk_exp[:], ended[:], AX_X, ALU.add))
            tab(V.tensor_scalar(exp_i[:], blk_exp[:], float(E - 1), None, ALU.min))
            V.tensor_tensor(wdiff[:], topv[:, :, 1], topv[:, :, 0], ALU.subtract).then_inc(wdiff_done, 1)

            dve.wait_ge(wexp_done, 1)
            V.tensor_scalar(wsum[:], wexp[:], 1.0, None, ALU.add).then_inc(wtop_done, 1)
            dve.wait_ge(wtop_done, 1)
            V.reciprocal(wtop[:, 0, :], wsum[:]).then_inc(wtop_done, 1)
            dve.wait_ge(wtop_done, 2)
            V.tensor_tensor(wtop[:, 1, :], wexp[:], wtop[:, 0, :], ALU.mult).then_inc(wtop_done, 1)

            def gate(b):
                dve.wait_ge(silu_done, b.n + 1)
                wait_past(dve, hT_done, b.n - 1)
                V.tensor_tensor(gated[:, b.par, :], act_h[:, b.par, :], ps_h[b.par][:, H:2 * H], ALU.mult)\
                    .then_inc(gated_done, 1)

            def copy_hT(b):
                dve.wait_ge(hT_done, b.n + 1)
                wait_past(dve, y_done, b.n - 1)
                V.tensor_copy(hT[:, b.par].rearrange("p c t -> p (c t)"), ps_hT[b.par][0:HA, 0:2 * P])\
                    .then_inc(hT_sb, 1)

            def copy_y(b):
                dve.wait_ge(y_done, b.n + 1)
                wait_past(dve, y_out[b.slot(RB)], b.round(RB) * 16)
                V.tensor_copy(y_sb[:, b.slot(RB), :], ps_y[b.par][:, 0:D]).then_inc(y_copied, 1)

            def ffn_body(do, b):
                do(copy_hT, b.plus(-1))
                do(gate, b)
                do(copy_y, b.plus(-2))

            blocks(dve, ffn_body, 0, 2)

            def combine(i, u):
                dve.wait_ge(y_back[u], i * 32 + 32)
                wait_past(dve, o_done, i * 8 + 2 * u)
                for a in range(2):
                    t = i * 8 + (2 * u + a)
                    V.scalar_tensor_tensor(y_half[:, a], y_in[:, u, 0, a], wtop[:, 0, bass.ds(t, 1)],
                                           xres[:, bass.ds(t, 1), :].rearrange("p a d -> p (a d)"),
                                           ALU.mult, ALU.add).then_inc(half_done, 1)
                wait_past(dve, o_stored[u], i * 16)
                for a in range(2):
                    t = i * 8 + (2 * u + a)
                    dve.wait_ge(half_done, t + 1)
                    V.scalar_tensor_tensor(o_sb[:, u, a], y_in[:, u, 1, a], wtop[:, 1, bass.ds(t, 1)], y_half[:, a],
                                           ALU.mult, ALU.add).then_inc(o_done, 1)

            for u in range(4):
                combine(0, u)
            with dve.Fori(1, T // 8) as i:
                for u in range(4):
                    combine(i, u)

        @block.scalar
        def _(act):
            S = nc.scalar

            def copy_xT(t):
                act.wait_ge(xT_done, t.n + 1)
                wait_past(act, v_done, t.n - 1)
                S.activation(xT[:, t.par], ps_tr[:, 0:3 * P], ACT.Copy).then_inc(xT_sb, 1)

            def copy_v(t):
                act.wait_ge(v_done, t.n + 1)
                wait_past(act, pv_done, t.times(2, -2))
                for o in range(2):
                    into = vst[64 * o:64 * o + 64, t.par].rearrange("p (j q) c -> p j q c", q=2)
                    for q in range(2):
                        ins = S.activation(into[:, :, q, 16 * q + 8 * o:16 * q + 8 * o + 8],
                                           ps_vo[64 * o:64 * o + 64, D:2 * D].rearrange(
                                               "p (j q d) -> p j q d", q=2, d=HD)[:, :, q], ACT.Copy)
                ins.then_inc(v_sb, 1)

            def transposed_halves(first):
                for o in range(2):
                    for b in range(2):
                        yield o, b, ps_tr[64 * o:64 * o + 64, first:first + D].rearrange(
                            "p (g b k) -> p g b k", g=G // 2, b=2)[:, :, b]

            def copy_kT(t):
                act.wait_ge(kqT_done, t.n + 1)
                wait_past(act, km_done, t.times(G, -G))
                for o, b, ps in transposed_halves(0):
                    ins = S.activation(kT[64 * b:64 * b + 64, t.par].rearrange("p (g o) k -> p g o k", o=2)[:, :, o],
                                       ps, ACT.Copy)
                ins.then_inc(kT_sb, 1)

            def copy_qT(t):
                act.wait_ge(kqT_done, t.n + 1)
                wait_past(act, l_done, t.times(G, -G))
                for o, b, ps in transposed_halves(D):
                    ins = S.activation(qbd[64 * b:64 * b + 64, t.par, :, 64 * b:64 * b + 64].rearrange(
                        "p (g o) k -> p g o k", o=2)[:, :, o], ps, ACT.Copy)
                ins.then_inc(qT_sb, 1)

            def exponential(t, g):
                act.wait_ge(shift_done, t.times(G, g + 1))
                wait_past(act, pt_done, t.times(G, g - 1))
                S.activation(expd[:, g % 2, :], shifted[:, g % 2, :], ACT.Exp, scale=SCALE).then_inc(exp_done, 1)

            def copy_pT(t, g):
                act.wait_ge(pt_done, t.times(G, g + 1))
                wait_past(act, pv_done, t.times(2, g // 2 - 1))
                S.activation(pT[:, g, :], ps_pt[g % 2][:], ACT.Copy).then_inc(pt_sb, 1)

            def copy_x1n(t):
                act.wait_ge(x2n_done, t.times(2, 1))
                wait_past(act, scattered[t.par], t.half * 32)
                S.activation(xs[:, t.par, 1, 0:D], xs[:, t.par, 0, 0:D], ACT.Copy).then_inc(x2c_done, 1)

            def copy_x2T(t):
                act.wait_ge(x2T_done, t.n + 1)
                wait_past(act, gate_done, t.n)
                S.activation(x2T[:], ps_tr[:, 0:D], ACT.Copy).then_inc(x2T_sb, 1)

            def weights(t, slot):
                for n in banks_of(t, slot):
                    if n % 2 == 0:
                        act.wait_ge(wt_done, n + 1)
                        into, ps = weight_copy(n)
                        S.activation(into, ps, ACT.Copy).then_inc(wt_sb[0], 1)

            def sines():
                act.wait_ge(rope_tables, 1)
                af = ang[:].rearrange("p a t c h -> p a t (c h)")
                S.activation(sin_t[:, :, 0, :], af[:, 0], ACT.Sin, scale=-1.0).then_inc(rope_tables, 1)
                S.activation(sin_t[:, :, 1, :], af[:, 0], ACT.Sin).then_inc(rope_tables, 1)
                S.activation(cos_t[:], af[:, 1], ACT.Sin).then_inc(rope_tables, 1)

            act.wait_ge(wg_done, 1)
            S.activation(wgT[:], ps_nd[:, 0:KC * E].rearrange("p (c e) -> p c e", c=KC), ACT.Copy)\
                .then_inc(wg_sb, 1)
            act.wait_ge(dve_const, N_DVE_CONST)

            def body(do, t):
                do(copy_pT, t, 0)
                do(copy_kT, t.plus(1))
                do(copy_qT, t.plus(1))
                do(exponential, t, 1)
                weights(t, 0)

                do(copy_v, t.plus(1))
                do(copy_pT, t, 1)
                do(exponential, t, 2)
                do(copy_xT, t.plus(3))
                if is_first(t, 3):
                    sines()
                weights(t, 1)

                do(copy_pT, t, 2)
                do(copy_x1n, t.plus(-2))
                do(exponential, t, 3)
                do(copy_x2T, t.plus(-2))
                weights(t, 2)

                do(copy_pT, t, 3)
                do(exponential, t.plus(1), 0)
                weights(t, 3)

            pipeline(act, body)

            pad_experts(act, E // 2, pad2_in)
            act.wait_ge(wdiff_done, 1)
            S.activation(wexp[:], wdiff[:], ACT.Exp).then_inc(wexp_done, 1)

            def copy_xbT(b):
                act.wait_ge(bT_done, b.n + 1)
                wait_past(act, h_done, b.n - 1)
                S.activation(xbT[:, b.par, :], ps_tr[:, 0:D], ACT.Copy).then_inc(bT_sb, 1)

            def silu(b):
                act.wait_ge(h_done, b.n + 1)
                wait_past(act, gated_done, b.n - 1)
                S.activation(act_h[:, b.par, :], ps_h[b.par][:, 0:H], ACT.Silu).then_inc(silu_done, 1)

            def ffn_body(do, b):
                do(silu, b)
                do(copy_xbT, b.plus(1))

            blocks(act, ffn_body, 1, 0)

            with act.Fori(0, T // 8) as i:
                for u in range(4):
                    act.wait_ge(o_done, i * 8 + (2 * u + 2))
                    act.dma_start(out_rows[bass.ds(i * (8 * P) + u * 2 * P, 2 * P), :].rearrange(
                        "(a p) d -> p a d", p=P), o_sb[:, u]).then_inc(o_stored[u], 16)
            for u in range(4):
                act.wait_ge(o_stored[u], 16 * (T // 8))

        @block.tensor
        def _(pe):
            M = nc.tensor

            def transpose_x(t):
                pe.wait_ge(xn_done, t.n + 1)
                pe.wait_ge(in_tile[t.par], t.half * 32 + 32)
                wait_past(pe, qT_sb, t.n - 1)
                for c in range(KC):
                    M.transpose(ps_tr[:, c * P:(c + 1) * P], xn[:, t.par, c * P:(c + 1) * P], ident[:])
                M.transpose(ps_tr[:, D:D + P], ctx_sb[:, t.par, :], ident[:]).then_inc(xT_done, 1)

            def project_qk(t):
                pe.wait_ge(xT_sb, t.n + 1)
                wait_past(pe, rope_done, t.n)
                for c in range(KC):
                    M.matmul(ps_qk[:, 0:D], xT[:, t.par, c * P:(c + 1) * P], wq_p[:, c, :],
                             start=(c == 0), stop=(c == KC - 1))
                M.matmul(ps_qk[:, D:2 * D], xT[:, t.par, D:D + P], wk_p[:], start=True, stop=True).then_inc(qk_done, 1)

            def project_v(t):
                pe.wait_ge(xT_sb, t.n + 1)
                wait_past(pe, x1_done, t.n - 2)
                for b in range(2):
                    for o in range(2):
                        ins = M.matmul(ps_vo[64 * o:64 * o + 64, D + b * P:D + (b + 1) * P],
                                       xT[:, t.par, D + 64 * b:D + 64 * b + 64], wv_p[:, o, :], start=True, stop=True)
                ins.then_inc(v_done, 1)

            def transpose_kq(t):
                pe.wait_ge(rot_done, t.n + 1)
                pe.wait_ge(xT_sb, upto(t.n + 2))
                wait_past(pe, x2T_sb, t.n - 3)
                for first, into in ((D, 0), (0, D)):
                    for c in range(KC):
                        ins = M.transpose(ps_tr[:, into + c * P:into + (c + 1) * P],
                                          rot[:, first + c * P:first + (c + 1) * P], ident[:])
                ins.then_inc(kqT_done, 1)

            def logits(t, g):
                pe.wait_ge(km_done, t.times(G, g + 1))
                if g == 0:
                    pe.wait_ge(qT_sb, t.n + 1)
                wait_past(pe, shift_done, t.times(G, g - 1))
                M.matmul(ps_l[g % 2][:], qbd[:, t.par, g, :], km[:, t.par, g].rearrange("p h k -> p (h k)"),
                         start=True, stop=True).then_inc(l_done, 1)

            def transpose_p(t, g):
                pe.wait_ge(exp_done, t.times(G, g + 1))
                wait_past(pe, pt_sb, t.times(G, g - 1))
                for j in range(G):
                    ins = M.transpose(ps_pt[g % 2][:, j * P:(j + 1) * P], expd[:, g % 2, j * P:(j + 1) * P], ident[:])
                ins.then_inc(pt_done, 1)

            def attend(t, c):
                pe.wait_ge(pt_sb, t.times(G, 2 * c + 2))
                if c == 0:
                    pe.wait_ge(v_sb, t.n + 1)
                    wait_past(pe, norm_done, t.n)
                probs = pT[:].rearrange("p g (j k) -> p (g j) k", k=P)
                for b in range(2):
                    for q in range(2):
                        for j in range(4):
                            pair = 8 * c + 2 * j + q
                            M.matmul(ps_nd[32 * j:32 * j + 32, c * P + 64 * b:c * P + 64 * b + 64],
                                     vst[:, t.par, 16 * b + pair, :], probs[:, pair, 64 * b:64 * b + 64],
                                     start=(q == 0), stop=(q == 1))
                for q in range(2):
                    for j in range(4):
                        ins = M.matmul(ps_nd[32 * j:32 * j + 32, D + c * P:D + (c + 1) * P], ones_pair[:, q, :],
                                       probs[:, 8 * c + 2 * j + q, :], start=(q == 0), stop=(q == 1))
                ins.then_inc(pv_done, 1)

            def project_out(t):
                pe.wait_ge(norm_done, t.n + 1)
                pe.wait_ge(v_sb, upto(t.n + 3))
                wait_past(pe, rank_read, t.n - 1)
                for c in range(KC):
                    ins = M.matmul(ps_vo[:, 0:D], attnT[:, c * P:(c + 1) * P], wout_sb[:, c, :],
                                   start=(c == 0), stop=(c == KC - 1))
                ins.then_inc(out_done, 1)

            def transpose_x1(t):
                pe.wait_ge(x2n_done, t.times(2, 1))
                pe.wait_ge(qT_sb, upto(t.n + 4))
                pe.wait_ge(xT_sb, upto(t.n + 6))
                for c in range(KC):
                    ins = M.transpose(ps_tr[:, c * P:(c + 1) * P], xs[:, t.par, 0, c * P:(c + 1) * P], ident[:])
                ins.then_inc(x2T_done, 1)

            def score(t):
                pe.wait_ge(x2T_sb, t.n + 1)
                pe.wait_ge(x1_done, upto(t.n + 2))
                pe.wait_ge(v_sb, upto(t.n + 5))
                wait_past(pe, rank_read, t.n)
                for c in range(KC):
                    ins = M.matmul(ps_vo[:, 0:E], x2T[:, c * P:(c + 1) * P], wgT[:, c, :],
                                   start=(c == 0), stop=(c == KC - 1))
                ins.then_inc(gate_done, 1)

            def rank(t):
                pe.wait_ge(top_done, t.n + 1)
                wait_past(pe, chosen_done, t.n)
                M.matmul(ps_vo[:, E:2 * E], tri[:], chosen[:], start=True, stop=False)
                M.matmul(ps_vo[:, E:2 * E], ones_bf[:], seen[:], start=False, stop=True).then_inc(rank_done, 1)

            def weights(t, slot):
                for n in banks_of(t, slot):
                    kind, e, c = weight_bank(n)
                    if n == 0:
                        pe.wait_ge(shift_done, T * G)
                        pe.wait_ge(pt_sb, T * G)
                        pe.wait_ge(wf1_in, 32)
                    if n == E * KC:
                        pe.wait_ge(wf3_in, 32)
                    if n == E * KC + E:
                        pe.wait_ge(wf2_in, 32)
                    if n >= 4:
                        pe.wait_ge(wt_sb[n % 2], (n - 4) // 2 + 1)
                    ps = wt_banks[n % 4]
                    if kind == 3:
                        for h in range(2):
                            for d in range(KC):
                                ins = M.transpose(ps[0:HA, h * D + d * P:h * D + (d + 1) * P],
                                                  w3_raw[:, d, e, h * HB:h * HB + HA], ident[:])
                    else:
                        wa, wb = (w1a[:], w1b[:]) if kind == 1 else (w2a, w2b)
                        M.transpose(ps[:, 0:P], wa[:, e, c * P:(c + 1) * P], ident[:])
                        ins = M.transpose(ps[:, P:H], wb[:, e, c * P:(c + 1) * P], ident[0:H - P, 0:H - P])
                    ins.then_inc(wt_done, 1)

            pe.wait_ge(pool_const, N_POOL_CONST)
            pe.wait_ge(w_in, 16 * N_W)
            for c in range(KC):
                ins = M.transpose(ps_nd[:, c * E:(c + 1) * E], wg_raw[:, c * P:(c + 1) * P], ident[0:E, 0:E])
            ins.then_inc(wg_done, 1)
            pe.wait_ge(wg_sb, 1)
            pe.wait_ge(dve_const, N_DVE_CONST)
            pe.wait_ge(wqk_ready, KC + 2)

            def body(do, t):
                do(logits, t, 2)
                do(transpose_p, t, 0)
                do(transpose_kq, t.plus(1))
                do(attend, t.plus(-1), 1)
                weights(t, 0)

                do(logits, t, 3)
                do(project_v, t.plus(1))
                do(transpose_p, t, 1)
                do(transpose_x, t.plus(3))
                weights(t, 1)

                do(logits, t.plus(1), 0)
                do(score, t.plus(-3))
                do(transpose_p, t, 2)
                do(attend, t, 0)
                do(transpose_x1, t.plus(-2))
                weights(t, 2)

                do(logits, t.plus(1), 1)
                do(transpose_p, t, 3)
                do(rank, t.plus(-3))
                do(project_qk, t.plus(3))
                do(project_out, t.plus(-1))
                weights(t, 3)

            pipeline(pe, body)
            pe.wait_ge(chosen_done, T)
            pe.wait_ge(x1_done, T)
            M.matmul(ps_vo[:, 0:E], ones_bf[:], seen[:], start=True, stop=True).then_inc(cnt_done, 1)

            def transpose_block(b):
                pe.wait_ge(blk_in[b.slot(RB)], b.round(RB) * 16 + 16)
                wait_past(pe, bT_sb, b.n)
                for c in range(KC):
                    ins = M.transpose(ps_tr[:, c * P:(c + 1) * P], xb[:, b.slot(RB), c * P:(c + 1) * P], ident[:])
                ins.then_inc(bT_done, 1)

            ahead = [pe.alloc_register(f"expert{n}") for n in range(2 * RB)]
            experts = []

            def load_experts(i):
                pe.load(ahead, exp_i[0:1, bass.ds(i * RB, 2 * RB)])
                experts[:] = [pe.snap(r, min_val=0, max_val=E - 1) for r in ahead]

            def expert_of(b):
                if isinstance(b.i, int):
                    return pe.value_load(exp_i[0:1, b.n:b.n + 1], min_val=0, max_val=E - 1)
                return experts[b.c]

            def hidden(b):
                e = expert_of(b)
                pe.wait_ge(bT_sb, b.n + 1)
                wait_past(pe, gated_done, b.n - 1)
                for c in range(KC):
                    ins = M.matmul(ps_h[b.par][:, 0:2 * H], xbT[:, b.par, c * P:(c + 1) * P],
                                   w12T[:, bass.ds(e, 1), c, :].rearrange("p a h -> p (a h)"),
                                   start=(c == 0), stop=(c == KC - 1))
                ins.then_inc(h_done, 1)

            def transpose_hidden(b):
                pe.wait_ge(gated_done, b.n + 1)
                wait_past(pe, hT_sb, b.n - 1)
                for c in range(2):
                    ins = M.transpose(ps_hT[b.par][0:HA, c * P:(c + 1) * P], gated[:, b.par, c * HB:c * HB + HA], ident[:])
                ins.then_inc(hT_done, 1)

            def result(b):
                e = expert_of(b)
                pe.wait_ge(hT_sb, b.n + 1)
                wait_past(pe, y_copied, b.n - 1)
                for c in range(2):
                    ins = M.matmul(ps_y[b.par][:, 0:D], hT[:, b.par, c, :],
                                   w3T[:, bass.ds(e, 1), c, :].rearrange("p a d -> p (a d)"),
                                   start=(c == 0), stop=(c == 1))
                ins.then_inc(y_done, 1)

            pe.wait_ge(wdiff_done, 1)
            pe.wait_ge(wt_sb[0], NWT // 2)
            pe.wait_ge(w3_zero, 1)

            def ffn_body(do, b):
                do(hidden, b)
                do(transpose_hidden, b.plus(-1))
                do(transpose_block, b.plus(1))
                do(result, b.plus(-2))

            blocks(pe, ffn_body, 1, 2, load_experts)
    return nc


_INS = ['x', 'ctx_1024', 'fside_BxSx2_0', 'L0_xattn_Wq', 'L0_xattn_Wkv', 'L0_xattn_Wout', 'L0_xattn_bout',
        'L0_ffn_Wg', 'L0_ffn_W1', 'L0_ffn_W2', 'L0_ffn_W3']


def kernel(**inputs):
    import numpy as _np
    import concourse.bacc as _bacc
    from concourse import mybir as _mybir
    from concourse.bass_utils import run_bass_kernel_spmd as _run

    nc = _bacc.Bacc("TRN2", target_bir_lowering=False, num_devices=1)
    arrays, args = {}, []
    for name in _INS:
        a = _np.ascontiguousarray(inputs[name])
        arrays[f"in_{name}_dram"] = a
        args.append(nc.dram_tensor(f"in_{name}_dram", a.shape, _mybir.dt.from_np(a.dtype), kind="ExternalInput").ap())
    args.append(nc.dram_tensor("out_0_dram", (64, 64, 256), _mybir.dt.float32, kind="ExternalOutput").ap())
    xattn_ffn_kernel(nc, *args)
    r = _run(nc, [arrays], core_ids=[0])
    return r.results[0]["out_0_dram"]
```

```python
import math
from contextlib import ExitStack

import numpy as np

import concourse.bass as bass
from concourse import mybir

P = 128
ALU = mybir.AluOpType
ACT = mybir.ActivationFunctionType
F32 = mybir.dt.float32
FR = mybir.dt.float32r
BF16 = mybir.dt.bfloat16
I32 = mybir.dt.int32
U32 = mybir.dt.uint32
AX_X = mybir.AxisListType.X
MAGIC = 1.5 * 2.0 ** 23
EPS = 1e-5


class Turn:

    def __init__(self, i, c, u=2):
        self.i, self.c, self.u = i, c, u

    def plus(self, d):
        return Turn(self.i, self.c + d, self.u)

    def times(self, m, d=0):
        return self.i * (self.u * m) + (self.c * m + d)

    @property
    def n(self):
        return self.times(1)

    def slot(self, ring):
        return self.c % ring

    def round(self, ring):
        return self.i * (self.u // ring) + self.c // ring

    @property
    def par(self):
        return self.slot(2)

    @property
    def half(self):
        return self.round(2)

    def within(self, end):
        return not isinstance(self.i, int) or 0 <= self.n < end


def xattn_ffn_kernel(nc, x, ctx_in, pos, Wq, Wkv, Wout, bout, Wg, W1, W2, W3, out):
    B, N, D = x.shape
    CD = ctx_in.shape[2]
    E, H, _ = W1.shape
    TOKENS = B * N
    T = TOKENS // P
    KC = D // P
    HEADS, HD = 32, 8
    GH = 8
    G = HEADS // GH
    GW = GH * HD
    SCALE = float(np.float32(1.0) / np.sqrt(np.float32(HD)))
    HA = 96
    HB = H - HA
    OVER = HA - HB
    RC = TOKENS + P
    NBLK = 2 * TOKENS // P + E - 1
    SPARE = E - 1
    RW = D + 1
    NOWHERE = 1 << 20
    assert N == 64 and P == 2 * N and T % 8 == 0 and CD == P and D == 2 * P

    x_rows = x.rearrange("b n d -> (b n) d")
    ctx_rows = ctx_in.rearrange("b n d -> (b n) d")
    out_rows = out.rearrange("b n d -> (b n) d")
    pos_rows = pos.rearrange("b n c -> (b n) c").rearrange("(t p) c -> p t c", p=P)
    routed = nc.dram_tensor("routed_rows", (E * RC + SPARE * P, RW), F32, kind="Internal").ap()
    results = nc.dram_tensor("result_rows", (2 * TOKENS, D), F32, kind="Internal").ap()

    with ExitStack() as es:
        def sb(name, shape, dt=F32):
            return es.enter_context(nc.sbuf_tensor(name, shape, dt))

        def sem(name):
            return es.enter_context(nc.semaphore(name))

        banks = [es.enter_context(nc.psum_tensor(f"bank{n}", [P, 512], F32)) for n in range(8)]
        ps_l, ps_pt, ps_qk, ps_vo, ps_nd, ps_tr = banks[0:2], banks[2:4], banks[4], banks[5], banks[6], banks[7]

        xres = sb("xres", [P, T, D])
        exp_i = sb("exp_i", [1, NBLK], I32)
        x_sb = sb("x_sb", [P, 2, D])
        ctx_sb = sb("ctx_sb", [P, 2, CD])
        xn = sb("xn", [P, 2, D])
        stats = sb("stats", [P, 2, 6])
        mv1 = sb("mv1", [P, 2, 2])
        rstd1 = sb("rstd1", [P, 2])
        mv2 = sb("mv2", [P, 2, 2])
        rstd2 = sb("rstd2", [P, 2])
        var_eps1 = sb("var_eps1", [P, 1])
        var_eps2 = sb("var_eps2", [P, 1])
        minus_half = sb("minus_half", [P, 1])
        rope_a = sb("rope_a", [P, 512])
        kT = sb("kT", [P, 2, G, N])
        qbd = sb("qbd", [P, 2, G, P])
        rowmax = sb("rowmax", [P, 2, GH])
        rden = sb("rden", [P, D])
        attnT = sb("attnT", [P, D])
        xs = sb("xs", [P, 2, 2, RW])
        x2T = sb("x2T", [P, D])
        top8 = sb("top8", [P, 8])
        idx8 = sb("idx8", [P, 8], U32)
        onehot = sb("onehot", [P, 2, E])
        chosen = sb("chosen", [P, E], BF16)
        seen = sb("seen", [P, E], BF16)
        place = sb("place", [P, E])
        place2 = sb("place2", [P, 2, E])
        slots = sb("slots", [P, 2, 2], I32)
        topv = sb("topv", [P, T, 2])
        ident = sb("ident", [P, P])
        tri = sb("tri", [P, P], BF16)
        ones_bf = sb("ones_bf", [P, P], BF16)
        mask32 = sb("mask32", [P, 32])
        mask = sb("mask", [P, GH])
        ones_pair = sb("ones_pair", [P, 2, 32])
        bout_sb = sb("bout_sb", [P, D])
        pos_sb = sb("pos_sb", [P, T, 2])
        ang = sb("ang", [P, 2, T, 2, 2])
        turns = sb("turns", [P, 2 * T * 4])
        cos_t = sb("cos_t", [P, T, 4])
        sin_t = sb("sin_t", [P, T, 2, 4])
        iota_e = sb("iota_e", [P, E])
        iota_ei = sb("iota_ei", [P, E], I32)
        region = sb("region", [P, E])
        dest_i = sb("dest_i", [P, T, 2], I32)
        dest = sb("dest", [P, T, 2])
        pad_row = sb("pad_row", [P, RW])
        wq_raw = sb("wq_raw", [P, KC, D])
        wkv_raw = sb("wkv_raw", [P, 2 * D])
        wq_p = sb("wq_p", [P, KC, D])
        wk_p = sb("wk_p", [P, D])
        wv_p = sb("wv_p", [P, 2, P])
        wout_sb = sb("wout_sb", [P, KC, D])
        wg_raw = sb("wg_raw", [E, D])
        wgT = sb("wgT", [P, KC, E])
        w12a = sb("w12a", [P, E, D])
        w12b = sb("w12b", [H - P, E, D])
        w12_hi = sb("w12_hi", [P, E, KC, 2 * H], FR)
        w3_raw = sb("w3_raw", [P, KC, E, H])
        w3_hi = sb("w3_hi", [HA, E, 2, D], FR)
        cntf = sb("cntf", [1, E])
        nblk = sb("nblk", [1, E])
        nblk2 = sb("nblk2", [1, E])
        skip = sb("skip", [1, E])
        blk_end = sb("blk_end", [1, E])
        onesrow = sb("onesrow", [1, E])
        jrow_i = sb("jrow_i", [1, NBLK], I32)
        jrow = sb("jrow", [1, NBLK])
        ended = sb("ended", [1, NBLK, E])
        ended_n = sb("ended_n", [1, NBLK, E])
        blk_exp = sb("blk_exp", [1, NBLK])
        blk_first = sb("blk_first", [1, NBLK])
        blk_row = sb("blk_row", [1, NBLK])
        cnt_i = sb("cnt_i", [1, E], I32)
        row_i = sb("row_i", [1, NBLK], I32)
        RB = 8
        xb = sb("xb", [P, RB, RW])
        act_h = sb("act_h", [P, 2, H])
        gated = sb("gated", [P, 2, H])
        blk_dest = sb("blk_dest", [P, RB], I32)
        wdiff = sb("wdiff", [P, T])
        wexp = sb("wexp", [P, T])
        wsum = sb("wsum", [P, T])
        wtop = sb("wtop", [P, 2, T])

        with ExitStack() as attention:
            def early(name, shape):
                return attention.enter_context(nc.sbuf_tensor(name, shape, F32))

            late = early("late", [P, 6144])
            km = early("km", [P, 2, G, GH, N])
            xT = early("xT", [P, 2, 3 * P])
            rope_b = early("rope_b", [P, 512])
            rot = early("rot", [P, 512])
        vst = late[:, 0:2048].rearrange("p (t v c) -> p t v c", t=2, c=32)
        shifted = late[:, 2048:3072].rearrange("p (a n) -> p a n", a=2)
        expd = late[:, 3072:4096].rearrange("p (a n) -> p a n", a=2)
        pT = late[:, 4096:6144].rearrange("p (g n) -> p g n", g=G)
        w12_lo = sb("w12_lo", [P, E, KC, 2 * H], FR)
        w3_lo = sb("w3_lo", [HA, E, 2, D], FR)
        x_hi = sb("x_hi", [P, 2, D], FR)
        x_lo = sb("x_lo", [P, 2, D], FR)
        h_hi = sb("h_hi", [HA, 2, 2, P], FR)
        h_lo = sb("h_lo", [HA, 2, 2, P], FR)

        wqk_in = sem("wqk_in")
        wqk_ready = sem("wqk_ready")
        pos_in = sem("pos_in")
        w_in = sem("w_in")
        wf1_in = sem("wf1_in")
        wf2_in = sem("wf2_in")
        wf3_in = sem("wf3_in")
        in_tile = [sem("in_even"), sem("in_odd")]
        pool_const = sem("pool_const")
        pool_step = sem("pool_step")
        dve_const = sem("dve_const")
        dve_step = sem("dve_step")
        rope_tables = sem("rope_tables")
        wt_done = sem("wt_done")
        waits_over = sem("waits_over")
        wt_hi = sem("wt_hi")
        wt_sb = sem("wt_sb")
        stats1_done, mv1_done, rstd1_done, xn_done, xb_done = (
            sem(s) for s in ("stats1_done", "mv1_done", "rstd1_done", "xn_done", "xb_done"))
        eps1_done, eps2_done = sem("eps1_done"), sem("eps2_done")
        xT_done, xT_sb, qk_done, v_done, v_sb = (sem(s) for s in ("xT_done", "xT_sb", "qk_done", "v_done", "v_sb"))
        rope_done, rot_done = sem("rope_done"), sem("rot_done")
        kqT_done, kT_sb, qT_sb, km_done = (sem(s) for s in ("kqT_done", "kT_sb", "qT_sb", "km_done"))
        l_done, max_done, shift_done, exp_done, pt_done, pt_sb, pv_done = (
            sem(s) for s in ("l_done", "max_done", "shift_done", "exp_done", "pt_done", "pt_sb", "pv_done"))
        rden_done, norm_done, out_done, x1_done = (sem(s) for s in ("rden_done", "norm_done", "out_done", "x1_done"))
        stats2_done, mv2_done, rstd2_done, x2n_done = (
            sem(s) for s in ("stats2_done", "mv2_done", "rstd2_done", "x2n_done"))
        x2c_done = sem("x2c_done")
        x2T_done, x2T_sb, gate_done, top_done, rank_done, rank_read, slot_done = (
            sem(s) for s in ("x2T_done", "x2T_sb", "gate_done", "top_done", "rank_done", "rank_read", "slot_done"))
        route_step = sem("route_step")
        chosen_done = sem("chosen_done")
        scattered = [sem("scattered_even"), sem("scattered_odd")]
        spare_in = sem("spare_in")
        cnt_done, cnt_i_done, tab_step, row_done, pad_in, pad2_in = (
            sem(s) for s in ("cnt_done", "cnt_i_done", "tab_step", "row_done", "pad_in", "pad2_in"))
        blk_in = [sem(f"blk_in{n}") for n in range(RB)]
        bT_hi, hT_hi = sem("bT_hi"), sem("hT_hi")
        bT_done, bT_sb, h_done, silu_done, gated_done, hT_done, hT_sb, y_done, y_copied = (
            sem(s) for s in ("bT_done", "bT_sb", "h_done", "silu_done", "gated_done", "hT_done", "hT_sb",
                             "y_done", "y_copied"))
        y_out = [sem(f"y_out{n}") for n in range(RB)]
        dest_done = sem("dest_done")
        wdiff_done, wexp_done, wtop_done = sem("wdiff_done"), sem("wexp_done"), sem("wtop_done")
        wg_done, wg_sb, w3_zero = sem("wg_done"), sem("wg_sb"), sem("w3_zero")
        y_back = [sem(f"y_back{n}") for n in range(4)]
        half_done, o_done = sem("half_done"), sem("o_done")
        o_stored = [sem(f"o_stored{n}") for n in range(4)]

        N_POOL_CONST, N_DVE_CONST, N_W = 9, 9, 3
        NWT = 2 * E * KC + E
        SLOT_BANKS = (0, 4, 4, 0, 4, 4)
        NWA = sum(SLOT_BANKS)
        NWB = NWT - 10
        wt_banks = [banks[0], banks[1], banks[2], banks[3]]
        ps_h, ps_y, ps_hT = banks[0:2], banks[2:4], banks[4:6]
        y_sb = w12a[:, 0:RB, :]
        y_in = km[:].rearrange("p u g (b h) k -> p (u g) (b h k)", b=2).rearrange(
            "p (v k) (a d) -> p v k a d", k=2, d=D)
        o_sb = late[:, 0:2048].rearrange("p (v a d) -> p v a d", v=4, a=2)
        y_half = rope_a[:].rearrange("p (a d) -> p a d", a=2)

        def weight_bank(n):
            if n < E * KC:
                return 1, n // KC, n % KC
            if n < E * KC + E:
                return 3, n - E * KC, 0
            n -= E * KC + E
            return 2, n // KC, n % KC

        def weight_copy(n):
            kind, e, c = weight_bank(n)
            ps = wt_banks[n % 4]
            if kind == 3:
                return (w3_hi[:, e].rearrange("p c d -> p (c d)"), w3_lo[:, e].rearrange("p c d -> p (c d)"),
                        ps[0:HA, 0:2 * D])
            first = 0 if kind == 1 else H
            return w12_hi[:, e, c, first:first + H], w12_lo[:, e, c, first:first + H], ps[:, 0:H]

        def is_first(t, ahead):
            return isinstance(t.i, int) and t.c == -ahead

        def banks_of(t, slot):
            if not isinstance(t.i, int) or t.c < T:
                return range(0)
            k = (t.c - T) * 4 + slot
            return range(sum(SLOT_BANKS[:k]), sum(SLOT_BANKS[:k + 1]))

        block = es.enter_context(nc.Block())

        def apart(eng):
            eng.sem_inc(waits_over, 1)

        def wait_past(eng, semaphore, value):
            if not (isinstance(value, int) and value <= 0):
                eng.wait_ge(semaphore, value)

        def pipeline(eng, body):
            def do(stage, t, *args):
                if t.within(T):
                    stage(t, *args)
            for c in range(-4, 5):
                body(do, Turn(0, c))
            with eng.Fori(2, (T - 6) // 2) as i:
                body(do, Turn(i, 1))
                body(do, Turn(i, 2))
            for c in range(T - 5, T + 3):
                body(do, Turn(0, c))

        def blocks(eng, body, after, prepare=None):
            def do(stage, b):
                if b.within(NBLK):
                    stage(b)
            for c in range(RB + 2):
                body(do, Turn(0, c, RB))
            rounds = (NBLK - 4) // RB
            with eng.Fori(1, rounds) as i:
                if prepare:
                    prepare(i * RB)
                for c in range(2, RB + 2):
                    body(do, Turn(i, c, RB))
            if prepare:
                prepare(rounds * RB)
            for c in range(rounds * RB + 2, NBLK + after):
                body(do, Turn(0, c, RB))

        def pad_experts(eng, first, padded):
            eng.wait_ge(cnt_i_done, 1)
            counts = [eng.alloc_register(f"count{first + n}") for n in range(E // 2)]
            eng.load(counts, cnt_i[0:1, first:first + E // 2])
            for n, reg in enumerate(counts):
                rows = eng.snap(reg, min_val=0, max_val=TOKENS)
                eng.dma_start(routed[bass.ds(rows + (first + n) * RC, P), :], pad_row[:]).then_inc(padded, 16)

        def last_weights(do_banks, stage, prepare=lambda: None):
            do_banks(range(NWA, NWA + 4))
            prepare()
            do_banks(range(NWA + 4, NWB))
            stage(Turn(0, 0, RB))
            do_banks(range(NWB, NWB + 4))
            stage(Turn(0, 1, RB))
            do_banks(range(NWB + 4, NWT))

        def upto(value):
            return min(value, T) if isinstance(value, int) else value

        @block.sync
        def _(sp):
            def load_tile(t):
                wait_past(sp, xb_done, t.n - 1)
                apart(sp)
                wait_past(sp, xT_done, t.n - 1)
                apart(sp)
                sp.dma_start(x_sb[:, t.par, :], x_rows[bass.ds(t.times(P), P), :]).then_inc(in_tile[t.par], 16)
                sp.dma_start(ctx_sb[:, t.par, :], ctx_rows[bass.ds(t.times(P), P), :]).then_inc(in_tile[t.par], 16)

            load_tile(Turn(0, 0))
            sp.dma_start(wkv_raw[:], Wkv).then_inc(wqk_in, 16)
            sp.dma_start(wq_raw[:], Wq.rearrange("(c p) n -> p c n", p=P)).then_inc(wqk_in, 16)
            sp.dma_start(pos_sb[:], pos_rows).then_inc(pos_in, 16)
            load_tile(Turn(0, 1))
            sp.dma_start(wg_raw[:], Wg).then_inc(w_in, 16)
            sp.dma_start(bout_sb[:], bout.rearrange("(a n) -> a n", a=1).broadcast_to([P, D])).then_inc(w_in, 16)
            sp.dma_start(wout_sb[:], Wout.rearrange("(c p) n -> p c n", p=P)).then_inc(w_in, 16)
            load_tile(Turn(0, 2))
            load_tile(Turn(0, 3))
            sp.dma_start(w12a[:], W1[:, 0:P, :].rearrange("e h d -> h e d")).then_inc(wf1_in, 16)
            sp.dma_start(w12b[:], W1[:, P:H, :].rearrange("e h d -> h e d")).then_inc(wf1_in, 16)
            for c in range(KC):
                sp.dma_start(w3_raw[:, c], W3[:, c * P:(c + 1) * P, :].rearrange("e p h -> p e h")).then_inc(wf3_in, 16)
            sp.wait_ge(pool_const, N_POOL_CONST)
            for s in range(SPARE):
                r0 = E * RC + s * P
                sp.dma_start(routed[r0:r0 + P, :], pad_row[:]).then_inc(spare_in, 16)
            with sp.Fori(2, T // 2) as i:
                load_tile(Turn(i, 0))
                load_tile(Turn(i, 1))

            sp.wait_ge(wt_done, E * KC)
            sp.dma_start(w12a[:], W2[:, 0:P, :].rearrange("e h d -> h e d")).then_inc(wf2_in, 16)
            sp.dma_start(w12b[:], W2[:, P:H, :].rearrange("e h d -> h e d")).then_inc(wf2_in, 16)
            pad_experts(sp, 0, pad_in)
            sp.wait_ge(row_done, 1)
            sp.wait_ge(pad_in, 16 * (E // 2))
            sp.wait_ge(pad2_in, 16 * (E // 2))
            sp.wait_ge(spare_in, 16 * SPARE)
            for par in range(2):
                sp.wait_ge(scattered[par], 32 * (T // 2))

            def load_block(b):
                wait_past(sp, bT_done, b.n - RB + 1)
                apart(sp)
                wait_past(sp, dest_done, b.n - RB + 1)
                apart(sp)
                row = sp.value_load(row_i[0:1, bass.ds(b.n, 1)], min_val=0, max_val=E * RC + (SPARE - 1) * P)
                sp.dma_start(xb[:, b.slot(RB), :], routed[bass.ds(row, P), :]).then_inc(blk_in[b.slot(RB)], 16)

            blocks(sp, lambda do, b: do(load_block, b), 0)

            for n in range(RB):
                sp.wait_ge(y_out[n], 16 * ((NBLK - n + RB - 1) // RB))
            back = results.rearrange("(k r) d -> k r d", k=2)

            def load_results(i, u):
                for k in range(2):
                    r0 = i * (8 * P) + u * 2 * P
                    sp.dma_start(y_in[:, u, k], back[k, bass.ds(r0, 2 * P), :].rearrange("(a p) d -> p a d", p=P))\
                        .then_inc(y_back[u], 16)

            for u in range(4):
                load_results(0, u)
            with sp.Fori(1, T // 8) as i:
                for u in range(4):
                    sp.wait_ge(o_done, i * 8 + (2 * u - 6))
                    apart(sp)
                    load_results(i, u)

        @block.gpsimd
        def _(pool):
            nc.gpsimd.memset(minus_half[:], -0.5).then_inc(pool_const, 1)
            nc.gpsimd.memset(ident[:], 0.0).then_inc(pool_step, 1)
            nc.gpsimd.memset(mask32[:], 1.0).then_inc(pool_step, 1)
            nc.gpsimd.memset(tri[:], 1.0).then_inc(pool_step, 1)
            nc.gpsimd.memset(pad_row[:], 0.0).then_inc(pool_step, 1)
            pool.wait_ge(pool_step, 4)
            nc.gpsimd.affine_select(out=ident[:], in_=ident[:], compare_op=ALU.not_equal, fill=1.0, base=0,
                                    pattern=[[-1, P]], channel_multiplier=1).then_inc(pool_const, 1)
            nc.gpsimd.affine_select(out=mask32[:], in_=mask32[:], compare_op=ALU.is_ge, fill=0.0, base=0,
                                    pattern=[[-4, 32]], channel_multiplier=1).then_inc(pool_step, 1)
            pool.wait_ge(pool_step, 5)
            nc.gpsimd.affine_select(out=mask32[:], in_=mask32[:], compare_op=ALU.is_ge, fill=0.0, base=3,
                                    pattern=[[4, 32]], channel_multiplier=-1).then_inc(pool_const, 1)
            nc.gpsimd.affine_select(out=tri[:], in_=tri[:], compare_op=ALU.is_gt, fill=0.0, base=0,
                                    pattern=[[1, P]], channel_multiplier=-1).then_inc(pool_const, 1)
            nc.gpsimd.iota(dest_i[:], [[P, T], [TOKENS, 2]], base=0, channel_multiplier=1).then_inc(pool_const, 1)
            nc.gpsimd.iota(iota_ei[:], [[1, E]], base=0, channel_multiplier=0).then_inc(pool_const, 1)
            nc.gpsimd.iota(jrow_i[:], [[1, NBLK]], base=0, channel_multiplier=0).then_inc(pool_const, 1)
            nc.gpsimd.memset(pad_row[:, D:RW], float(NOWHERE)).then_inc(pool_const, 1)
            nc.gpsimd.memset(onesrow[:], 1.0).then_inc(pool_const, 1)

            def rstd_of_x(t):
                pool.wait_ge(mv1_done, t.n + 1)
                wait_past(pool, rstd1_done, t.n)
                apart(pool)
                nc.gpsimd.tensor_scalar(var_eps1[:], mv1[:, t.par, 1:2], EPS, None, ALU.add).then_inc(eps1_done, 1)
                pool.wait_ge(eps1_done, t.n + 1)
                wait_past(pool, xn_done, t.n - 1)
                nc.gpsimd.tensor_tensor(rstd1[:, t.par:t.par + 1], var_eps1[:], minus_half[:], ALU.pow)\
                    .then_inc(rstd1_done, 1)

            def rstd_of_x1(t):
                pool.wait_ge(mv2_done, t.n + 1)
                wait_past(pool, rstd2_done, t.n)
                apart(pool)
                nc.gpsimd.tensor_scalar(var_eps2[:], mv2[:, t.par, 1:2], EPS, None, ALU.add).then_inc(eps2_done, 1)
                pool.wait_ge(eps2_done, t.n + 1)
                wait_past(pool, x2n_done, t.times(2))
                nc.gpsimd.tensor_tensor(rstd2[:, t.par:t.par + 1], var_eps2[:], minus_half[:], ALU.pow)\
                    .then_inc(rstd2_done, 1)

            def normalise_x(t):
                pool.wait_ge(rstd1_done, t.n + 1)
                wait_past(pool, xT_done, t.n - 1)
                apart(pool)
                nc.gpsimd.tensor_scalar(xn[:, t.par, :], x_sb[:, t.par, :], mv1[:, t.par, 0:1],
                                        rstd1[:, t.par:t.par + 1], ALU.subtract, ALU.mult).then_inc(xn_done, 1)

            def add_bias(t):
                pool.wait_ge(w_in, 16 * N_W)
                nc.gpsimd.tensor_tensor(xres[:, bass.ds(t.n, 1), :].rearrange("p a d -> p (a d)"),
                                        x_sb[:, t.par, :], bout_sb[:], ALU.add).then_inc(xb_done, 1)

            def rotate(t):
                pool.wait_ge(rope_done, t.n + 1)
                wait_past(pool, kqT_done, t.n)
                nc.gpsimd.tensor_tensor(rot[:], rope_a[:], rope_b[:], ALU.add).then_inc(rot_done, 1)

            def mask_keys(t, first):
                pool.wait_ge(kT_sb, t.n + 1)
                wait_past(pool, l_done, t.times(G, -G))
                for g in range(first, first + 2):
                    nc.gpsimd.tensor_tensor(km[:, t.par, g], kT[:, t.par, g].unsqueeze(1).broadcast_to([P, GH, N]),
                                            mask[:].unsqueeze(2).broadcast_to([P, GH, N]), ALU.mult)\
                        .then_inc(km_done, 1)

            def scatter(t):
                pool.wait_ge(slot_done, t.n + 1)
                pool.wait_ge(x2c_done, t.n + 1)
                apart(pool)
                for k in range(2):
                    nc.gpsimd.indirect_dma_start(
                        routed[:, :], bass.IndirectOffsetOnAxis(ap=slots[:, t.par, k:k + 1], axis=0),
                        xs[:, t.par, k, :], None).then_inc(scattered[t.par], 16)

            pool.wait_ge(dve_const, N_DVE_CONST)

            def body(do, t):
                do(mask_keys, t.plus(1), 0)
                do(rstd_of_x1, t.plus(-2))
                do(mask_keys, t.plus(1), 2)
                do(rotate, t.plus(2))
                do(rstd_of_x, t.plus(4))
                do(normalise_x, t.plus(4))
                do(add_bias, t.plus(4))
                do(scatter, t.plus(-3))

            pipeline(pool, body)

            def take_dest(b):
                pool.wait_ge(blk_in[b.slot(RB)], b.round(RB) * 16 + 16)
                wait_past(pool, y_out[b.slot(RB)], b.round(RB) * 16)
                apart(pool)
                nc.gpsimd.tensor_copy(blk_dest[:, b.slot(RB):b.slot(RB) + 1], xb[:, b.slot(RB), D:RW])\
                    .then_inc(dest_done, 1)

            def store_block(b):
                pool.wait_ge(y_copied, b.n + 1)
                pool.wait_ge(dest_done, b.n + 1)
                apart(pool)
                nc.gpsimd.indirect_dma_start(
                    results[:, :], bass.IndirectOffsetOnAxis(ap=blk_dest[:, b.slot(RB):b.slot(RB) + 1], axis=0),
                    y_sb[:, b.slot(RB), :], None, bounds_check=2 * TOKENS - 1, oob_is_err=False)\
                    .then_inc(y_out[b.slot(RB)], 16)

            pool.wait_ge(wt_sb, E * KC + E)
            for w3 in (w3_hi, w3_lo):
                nc.gpsimd.memset(w3[0:OVER, :, 1, :].bitcast(F32), 0.0).then_inc(w3_zero, 1)

            def ffn_body(do, b):
                do(take_dest, b)
                do(store_block, b.plus(-2))

            blocks(pool, ffn_body, 2)

        @block.vector
        def _(dve):
            V = nc.vector

            def stats_of_x(t):
                dve.wait_ge(in_tile[t.par], t.half * 32 + 32)
                wait_past(dve, mv1_done, t.n)
                apart(dve)
                V.bn_stats(stats[:, 0, :], x_sb[:, t.par, :]).then_inc(stats1_done, 1)

            def mean_of_x(t):
                dve.wait_ge(stats1_done, t.n + 1)
                wait_past(dve, xn_done, t.n - 1)
                apart(dve)
                V.bn_aggr(mv1[:, t.par, :], stats[:, 0, :]).then_inc(mv1_done, 1)

            def rope(t):
                dve.wait_ge(qk_done, t.n + 1)
                if is_first(t, 0):
                    dve.wait_ge(rope_tables, 4)
                wait_past(dve, rot_done, t.n)
                cos = cos_t[:, bass.ds(t.n, 1), :].rearrange("p a c -> p (a c)")
                V.tensor_tensor(rope_a[:].rearrange("p (s c) -> p s c", c=4),
                                ps_qk[:].rearrange("p (s c) -> p s c", c=4),
                                cos.unsqueeze(1).broadcast_to([P, P, 4]), ALU.mult)
                for i in range(2):
                    sn = sin_t[:, bass.ds(t.n, 1), i, :].rearrange("p a c -> p (a c)")
                    o = rope_b[:].rearrange("p (s i h c) -> p s i h c", s=2 * G, i=2, c=4)[:, :, i]
                    q = ps_qk[:].rearrange("p (s i h c) -> p s i h c", s=2 * G, i=2, c=4)[:, :, 1 - i]
                    ins = V.tensor_tensor(o, q, sn.unsqueeze(1).unsqueeze(1).broadcast_to([P, 2 * G, GH, 4]), ALU.mult)
                ins.then_inc(rope_done, 1)

            def grouped_logits(g):
                return ps_l[g % 2][:].rearrange("p (h k) -> p h k", k=N)

            def peak(t, g):
                dve.wait_ge(l_done, t.times(G, g + 1))
                wait_past(dve, shift_done, t.times(G, g - 1))
                V.tensor_reduce(rowmax[:, g % 2, :], grouped_logits(g), AX_X, ALU.max).then_inc(max_done, 1)

            def shift(t, g):
                dve.wait_ge(max_done, t.times(G, g + 1))
                wait_past(dve, exp_done, t.times(G, g - 1))
                V.tensor_tensor(shifted[:, g % 2, :].rearrange("p (h k) -> p h k", k=N), grouped_logits(g),
                                rowmax[:, g % 2, :].unsqueeze(2).broadcast_to([P, GH, N]), ALU.subtract)\
                    .then_inc(shift_done, 1)

            def invert_sums(t):
                dve.wait_ge(pv_done, t.times(2, 2))
                wait_past(dve, norm_done, t.n)
                V.reciprocal(rden[:], ps_nd[:, D:2 * D]).then_inc(rden_done, 1)

            def normalise_attn(t):
                dve.wait_ge(rden_done, t.n + 1)
                wait_past(dve, out_done, t.n)
                V.tensor_tensor(attnT[:], ps_nd[:, 0:D], rden[:], ALU.mult).then_inc(norm_done, 1)

            def row(t):
                return xres[:, bass.ds(t.n, 1), :].rearrange("p a d -> p (a d)")

            def residual(t):
                dve.wait_ge(out_done, t.n + 1)
                dve.wait_ge(xb_done, t.n + 1)
                V.tensor_tensor(row(t), ps_vo[:, 0:D], row(t), ALU.add).then_inc(x1_done, 1)

            def stats_of_x1(t):
                dve.wait_ge(x1_done, t.n + 1)
                wait_past(dve, mv2_done, t.n)
                apart(dve)
                V.bn_stats(stats[:, 1, :], row(t)).then_inc(stats2_done, 1)

            def mean_of_x1(t):
                dve.wait_ge(stats2_done, t.n + 1)
                wait_past(dve, x2n_done, t.times(2))
                apart(dve)
                V.bn_aggr(mv2[:, t.par, :], stats[:, 1, :]).then_inc(mv2_done, 1)

            def normalise_x1(t):
                dve.wait_ge(rstd2_done, t.n + 1)
                wait_past(dve, scattered[t.par], t.half * 32)
                wait_past(dve, x2T_done, t.n)
                V.tensor_scalar(xs[:, t.par, 0, 0:D], row(t), mv2[:, t.par, 0:1], rstd2[:, t.par:t.par + 1],
                                ALU.subtract, ALU.mult).then_inc(x2n_done, 1)
                V.tensor_copy(xs[:, t.par, :, D:RW],
                              dest[:, bass.ds(t.n, 1), :].rearrange("p a k -> p (a k)").unsqueeze(2))\
                    .then_inc(x2n_done, 1)

            def best_scores(t):
                dve.wait_ge(gate_done, t.n + 1)
                wait_past(dve, slot_done, t.n)
                apart(dve)
                V.max(top8[:], ps_vo[:, 0:E]).then_inc(route_step, 1)

            def best_experts(t):
                dve.wait_ge(route_step, t.times(4, 1))
                apart(dve)
                V.max_index(idx8[:], top8[:], ps_vo[:, 0:E]).then_inc(route_step, 1)
                V.tensor_copy(topv[:, bass.ds(t.n, 1), :].rearrange("p a k -> p (a k)"), top8[:, 0:2])

            def mark_choices(t):
                dve.wait_ge(route_step, t.times(4, 2))
                V.tensor_tensor(onehot[:], iota_e[:].unsqueeze(1).broadcast_to([P, 2, E]),
                                idx8[:, 0:2].unsqueeze(2).broadcast_to([P, 2, E]), ALU.is_equal).then_inc(route_step, 1)

            def join_choices(t):
                dve.wait_ge(route_step, t.times(4, 3))
                wait_past(dve, rank_done, t.n)
                V.tensor_tensor(chosen[:], onehot[:, 0, :], onehot[:, 1, :], ALU.add).then_inc(top_done, 1)

            def place_tokens(t):
                dve.wait_ge(rank_done, t.n + 1)
                wait_past(dve, chosen_done, t.n)
                V.tensor_tensor(place[:], ps_vo[:, E:2 * E], region[:], ALU.add).then_inc(rank_read, 1)
                V.tensor_tensor(seen[:], seen[:], chosen[:], ALU.add).then_inc(chosen_done, 1)

            def select_places(t):
                dve.wait_ge(rank_read, t.n + 1)
                V.tensor_tensor(place2[:], onehot[:], place[:].unsqueeze(1).broadcast_to([P, 2, E]), ALU.mult)\
                    .then_inc(route_step, 1)

            def set_slots(t):
                dve.wait_ge(route_step, t.times(4, 4))
                with nc.allow_low_precision(reason="sums of one row number and zeros"):
                    V.tensor_reduce(slots[:, t.par, :], place2[:], AX_X, ALU.add).then_inc(slot_done, 1)

            steps = [0]

            def step(ins):
                steps[0] += 1
                ins.then_inc(dve_step, 1)
                dve.wait_ge(dve_step, steps[0])

            V.memset(qbd[:], 0.0).then_inc(dve_const, 1)
            V.memset(vst, 0.0).then_inc(dve_const, 1)
            V.memset(seen[:], 0.0).then_inc(dve_const, 1)
            V.memset(ones_bf[:], 1.0).then_inc(dve_const, 1)
            step(V.memset(ones_pair[:], 0.0))
            for par in range(2):
                for h in range(2):
                    ins = V.memset(ones_pair[64 * h:64 * h + 64, par, 16 * par + 8 * h:16 * par + 8 * h + 8], 1.0)
            ins.then_inc(dve_const, 1)
            dve.wait_ge(pool_const, N_POOL_CONST)
            V.tensor_reduce(mask[:], mask32[:].rearrange("p (a h) -> p h a", h=GH), AX_X, ALU.add)\
                .then_inc(dve_const, 1)
            step(V.tensor_copy(iota_e[:], iota_ei[:]))
            V.tensor_scalar(region[:], iota_e[:], float(RC), None, ALU.mult).then_inc(dve_const, 1)
            V.tensor_copy(jrow[:], jrow_i[:]).then_inc(dve_const, 1)
            V.tensor_copy(dest[:], dest_i[:]).then_inc(dve_const, 1)

            def prepare():
                dve.wait_ge(wqk_in, 32)
                for c in range(KC):
                    V.tensor_copy(wq_p[:, c].rearrange("p (g i m) -> p g i m", g=G, i=2),
                                  wq_raw[:, c].rearrange("p (g m i) -> p g i m", g=G, i=2)).then_inc(wqk_ready, 1)
                V.tensor_copy(wk_p[:].rearrange("p (g i m) -> p g i m", g=G, i=2),
                              wkv_raw[:, 0:D].rearrange("p (g m i) -> p g i m", g=G, i=2)).then_inc(wqk_ready, 1)
                V.tensor_copy(wv_p[:].rearrange("p o (h d) -> p o h d", d=HD),
                              wkv_raw[:, D:2 * D].rearrange("p (h o d) -> p o h d", o=2, d=HD)).then_inc(wqk_ready, 1)
                dve.wait_ge(pos_in, 16)
                step(V.tensor_copy(ang[:, 0, :, :, 0], pos_sb[:]))
                step(V.tensor_scalar(ang[:, 0, :, :, 1], pos_sb[:], 10000.0 ** -0.5, None, ALU.mult))
                step(V.tensor_scalar(ang[:, 1], ang[:, 0], math.pi / 2, None, ALU.add))
                af = ang[:].rearrange("p a t c h -> p (a t c h)")
                step(V.tensor_scalar(turns[:], af, 1 / (2 * math.pi), MAGIC, ALU.mult, ALU.add))
                step(V.tensor_scalar(turns[:], turns[:], MAGIC, None, ALU.subtract))
                step(V.scalar_tensor_tensor(af, turns[:], -6.28125, af, ALU.mult, ALU.add))
                step(V.scalar_tensor_tensor(af, turns[:], -(2 * math.pi - 6.28125), af, ALU.mult, ALU.add))
                V.tensor_scalar(af, af, 3.1415925, -3.1415925, ALU.min, ALU.max).then_inc(rope_tables, 1)

            def weights(t, slot):
                split_weights(banks_of(t, slot))

            def split_weights(which):
                for n in which:
                    if n == 0:
                        dve.wait_ge(pv_done, 2 * T)
                    dve.wait_ge(wt_hi, n + 1)
                    hi, lo, ps = weight_copy(n)
                    V.tensor_tensor(lo, ps, hi.bitcast(F32), ALU.subtract).then_inc(wt_sb, 1)

            def body(do, t):
                do(peak, t, 1)
                do(residual, t.plus(-2))
                do(shift, t, 1)
                do(stats_of_x1, t.plus(-2))
                do(rope, t.plus(2))
                do(mean_of_x1, t.plus(-2))
                weights(t, 0)

                do(peak, t, 2)
                do(shift, t, 2)
                do(invert_sums, t.plus(-1))
                do(normalise_x1, t.plus(-2))
                do(normalise_attn, t.plus(-1))
                weights(t, 1)

                do(peak, t, 3)
                do(shift, t, 3)
                do(best_scores, t.plus(-3))
                do(stats_of_x, t.plus(4))
                do(best_experts, t.plus(-3))
                do(mean_of_x, t.plus(4))
                if is_first(t, 4):
                    prepare()
                do(mark_choices, t.plus(-3))
                weights(t, 2)

                do(peak, t.plus(1), 0)
                do(join_choices, t.plus(-3))
                do(shift, t.plus(1), 0)
                do(place_tokens, t.plus(-3))
                do(select_places, t.plus(-3))
                do(set_slots, t.plus(-3))
                weights(t, 3)

            pipeline(dve, body)

            dve.wait_ge(cnt_done, 1)
            tabs = [0]

            def tab(ins):
                tabs[0] += 1
                ins.then_inc(tab_step, 1)
                dve.wait_ge(tab_step, tabs[0])

            tab(V.tensor_copy(cntf[:], ps_vo[0:1, 0:E]))
            V.tensor_copy(cnt_i[:], cntf[:]).then_inc(cnt_i_done, 1)
            tab(V.tensor_scalar(nblk[:], cntf[:], 1.0 / P, (P - 1) / P - 0.5 + 0.5 / P, ALU.mult, ALU.add))
            tab(V.tensor_scalar(nblk[:], nblk[:], MAGIC, None, ALU.add))
            tab(V.tensor_scalar(nblk2[:], nblk[:], MAGIC, None, ALU.subtract))
            V.tensor_scalar(skip[:], nblk2[:], -float(P), float(RC), ALU.mult, ALU.add)
            tab(V.tensor_tensor_scan(blk_end[:], onesrow[:], nblk2[:], 0.0, ALU.mult, ALU.add))
            je = [1, NBLK, E]
            tab(V.tensor_tensor(ended[:], jrow[:].unsqueeze(2).broadcast_to(je),
                                blk_end[:].unsqueeze(1).broadcast_to(je), ALU.is_ge))
            tab(V.tensor_tensor(ended_n[:], ended[:], skip[:].unsqueeze(1).broadcast_to(je), ALU.mult))
            tab(V.tensor_reduce(blk_first[:], ended_n[:], AX_X, ALU.add))
            tab(V.scalar_tensor_tensor(blk_row[:], jrow[:], float(P), blk_first[:], ALU.mult, ALU.add))
            V.tensor_copy(row_i[:], blk_row[:]).then_inc(row_done, 1)
            tab(V.tensor_reduce(blk_exp[:], ended[:], AX_X, ALU.add))
            tab(V.tensor_scalar(exp_i[:], blk_exp[:], float(E - 1), None, ALU.min))
            V.tensor_tensor(wdiff[:], topv[:, :, 1], topv[:, :, 0], ALU.subtract).then_inc(wdiff_done, 1)

            def gate(b):
                dve.wait_ge(silu_done, b.n + 1)
                wait_past(dve, hT_done, b.n - 1)
                V.tensor_tensor(gated[:, b.par, :], act_h[:, b.par, :], ps_h[b.par][:, H:2 * H], ALU.mult)\
                    .then_inc(gated_done, 1)

            def split_hT(b):
                dve.wait_ge(hT_hi, b.n + 1)
                V.tensor_tensor(h_lo[:, b.par].rearrange("p c t -> p (c t)"), ps_hT[b.par][0:HA, 0:2 * P],
                                h_hi[:, b.par].rearrange("p c t -> p (c t)").bitcast(F32), ALU.subtract).then_inc(hT_sb, 1)

            def split_xbT(b):
                dve.wait_ge(bT_hi, b.n + 1)
                V.tensor_tensor(x_lo[:, b.par, :], ps_tr[:, 0:D], x_hi[:, b.par, :].bitcast(F32), ALU.subtract).then_inc(bT_sb, 1)

            def copy_y(b):
                dve.wait_ge(y_done, b.n + 1)
                wait_past(dve, y_out[b.slot(RB)], b.round(RB) * 16)
                V.tensor_copy(y_sb[:, b.slot(RB), :], ps_y[b.par][:, 0:D]).then_inc(y_copied, 1)

            def ffn_body(do, b):
                do(gate, b)
                do(split_hT, b.plus(-1))
                do(split_xbT, b.plus(2))
                do(copy_y, b.plus(-2))

            last_weights(split_weights, split_xbT)
            dve.wait_ge(wexp_done, 1)
            V.tensor_scalar(wsum[:], wexp[:], 1.0, None, ALU.add).then_inc(wtop_done, 1)
            dve.wait_ge(wtop_done, 1)
            V.reciprocal(wtop[:, 0, :], wsum[:]).then_inc(wtop_done, 1)
            dve.wait_ge(wtop_done, 2)
            V.tensor_tensor(wtop[:, 1, :], wexp[:], wtop[:, 0, :], ALU.mult).then_inc(wtop_done, 1)
            blocks(dve, ffn_body, 2)

            def combine(i, u):
                dve.wait_ge(y_back[u], i * 32 + 32)
                wait_past(dve, o_done, i * 8 + 2 * u)
                for a in range(2):
                    t = i * 8 + (2 * u + a)
                    V.scalar_tensor_tensor(y_half[:, a], y_in[:, u, 0, a], wtop[:, 0, bass.ds(t, 1)],
                                           xres[:, bass.ds(t, 1), :].rearrange("p a d -> p (a d)"),
                                           ALU.mult, ALU.add).then_inc(half_done, 1)
                wait_past(dve, o_stored[u], i * 16)
                for a in range(2):
                    t = i * 8 + (2 * u + a)
                    dve.wait_ge(half_done, t + 1)
                    V.scalar_tensor_tensor(o_sb[:, u, a], y_in[:, u, 1, a], wtop[:, 1, bass.ds(t, 1)], y_half[:, a],
                                           ALU.mult, ALU.add).then_inc(o_done, 1)

            for u in range(4):
                combine(0, u)
            with dve.Fori(1, T // 8) as i:
                for u in range(4):
                    combine(i, u)

        @block.scalar
        def _(act):
            S = nc.scalar

            def copy_xT(t):
                act.wait_ge(xT_done, t.n + 1)
                wait_past(act, v_done, t.n - 1)
                S.activation(xT[:, t.par], ps_tr[:, 0:3 * P], ACT.Copy).then_inc(xT_sb, 1)

            def copy_v(t):
                act.wait_ge(v_done, t.n + 1)
                wait_past(act, pv_done, t.times(2, -2))
                for o in range(2):
                    into = vst[64 * o:64 * o + 64, t.par].rearrange("p (j q) c -> p j q c", q=2)
                    for q in range(2):
                        ins = S.activation(into[:, :, q, 16 * q + 8 * o:16 * q + 8 * o + 8],
                                           ps_vo[64 * o:64 * o + 64, D:2 * D].rearrange(
                                               "p (j q d) -> p j q d", q=2, d=HD)[:, :, q], ACT.Copy)
                ins.then_inc(v_sb, 1)

            def transposed_halves(first):
                for o in range(2):
                    for b in range(2):
                        yield o, b, ps_tr[64 * o:64 * o + 64, first:first + D].rearrange(
                            "p (g b k) -> p g b k", g=G // 2, b=2)[:, :, b]

            def copy_kT(t):
                act.wait_ge(kqT_done, t.n + 1)
                wait_past(act, km_done, t.times(G, -G))
                for o, b, ps in transposed_halves(0):
                    ins = S.activation(kT[64 * b:64 * b + 64, t.par].rearrange("p (g o) k -> p g o k", o=2)[:, :, o],
                                       ps, ACT.Copy)
                ins.then_inc(kT_sb, 1)

            def copy_qT(t):
                act.wait_ge(kqT_done, t.n + 1)
                wait_past(act, l_done, t.times(G, -G))
                for o, b, ps in transposed_halves(D):
                    ins = S.activation(qbd[64 * b:64 * b + 64, t.par, :, 64 * b:64 * b + 64].rearrange(
                        "p (g o) k -> p g o k", o=2)[:, :, o], ps, ACT.Copy)
                ins.then_inc(qT_sb, 1)

            def exponential(t, g):
                act.wait_ge(shift_done, t.times(G, g + 1))
                wait_past(act, pt_done, t.times(G, g - 1))
                S.activation(expd[:, g % 2, :], shifted[:, g % 2, :], ACT.Exp, scale=SCALE).then_inc(exp_done, 1)

            def copy_pT(t, g):
                act.wait_ge(pt_done, t.times(G, g + 1))
                wait_past(act, pv_done, t.times(2, g // 2 - 1))
                S.activation(pT[:, g, :], ps_pt[g % 2][:], ACT.Copy).then_inc(pt_sb, 1)

            def copy_x1n(t):
                act.wait_ge(x2n_done, t.times(2, 1))
                wait_past(act, scattered[t.par], t.half * 32)
                S.activation(xs[:, t.par, 1, 0:D], xs[:, t.par, 0, 0:D], ACT.Copy).then_inc(x2c_done, 1)

            def copy_x2T(t):
                act.wait_ge(x2T_done, t.n + 1)
                wait_past(act, gate_done, t.n)
                S.activation(x2T[:], ps_tr[:, 0:D], ACT.Copy).then_inc(x2T_sb, 1)

            def weights(t, slot):
                copy_weights(banks_of(t, slot))

            def copy_weights(which):
                for n in which:
                    act.wait_ge(wt_done, n + 1)
                    hi, _, ps = weight_copy(n)
                    S.activation(hi, ps, ACT.Copy).then_inc(wt_hi, 1)

            def sines():
                act.wait_ge(rope_tables, 1)
                af = ang[:].rearrange("p a t c h -> p a t (c h)")
                S.activation(sin_t[:, :, 0, :], af[:, 0], ACT.Sin, scale=-1.0).then_inc(rope_tables, 1)
                S.activation(sin_t[:, :, 1, :], af[:, 0], ACT.Sin).then_inc(rope_tables, 1)
                S.activation(cos_t[:], af[:, 1], ACT.Sin).then_inc(rope_tables, 1)

            act.wait_ge(wg_done, 1)
            S.activation(wgT[:], ps_nd[:, 0:KC * E].rearrange("p (c e) -> p c e", c=KC), ACT.Copy)\
                .then_inc(wg_sb, 1)
            act.wait_ge(dve_const, N_DVE_CONST)

            def body(do, t):
                do(copy_pT, t, 0)
                do(copy_kT, t.plus(1))
                do(copy_qT, t.plus(1))
                do(exponential, t, 1)
                weights(t, 0)

                do(copy_v, t.plus(1))
                do(copy_pT, t, 1)
                do(exponential, t, 2)
                do(copy_xT, t.plus(3))
                if is_first(t, 3):
                    sines()
                weights(t, 1)

                do(copy_pT, t, 2)
                do(copy_x1n, t.plus(-2))
                do(exponential, t, 3)
                do(copy_x2T, t.plus(-2))
                weights(t, 2)

                do(copy_pT, t, 3)
                do(exponential, t.plus(1), 0)
                weights(t, 3)

            pipeline(act, body)

            pad_experts(act, E // 2, pad2_in)
            def copy_xbT(b):
                act.wait_ge(bT_done, b.n + 1)
                wait_past(act, h_done, b.n - 1)
                S.activation(x_hi[:, b.par, :], ps_tr[:, 0:D], ACT.Copy).then_inc(bT_hi, 1)

            def copy_hT(b):
                act.wait_ge(hT_done, b.n + 1)
                wait_past(act, y_done, b.n - 1)
                S.activation(h_hi[:, b.par].rearrange("p c t -> p (c t)"), ps_hT[b.par][0:HA, 0:2 * P], ACT.Copy)\
                    .then_inc(hT_hi, 1)

            def silu(b):
                act.wait_ge(h_done, b.n + 1)
                wait_past(act, gated_done, b.n - 1)
                S.activation(act_h[:, b.par, :], ps_h[b.par][:, 0:H], ACT.Silu).then_inc(silu_done, 1)

            def ffn_body(do, b):
                do(silu, b)
                do(copy_hT, b.plus(-1))
                do(copy_xbT, b.plus(2))

            last_weights(copy_weights, copy_xbT)
            act.wait_ge(wdiff_done, 1)
            S.activation(wexp[:], wdiff[:], ACT.Exp).then_inc(wexp_done, 1)
            blocks(act, ffn_body, 1)

            with act.Fori(0, T // 8) as i:
                for u in range(4):
                    act.wait_ge(o_done, i * 8 + (2 * u + 2))
                    act.dma_start(out_rows[bass.ds(i * (8 * P) + u * 2 * P, 2 * P), :].rearrange(
                        "(a p) d -> p a d", p=P), o_sb[:, u]).then_inc(o_stored[u], 16)
            for u in range(4):
                act.wait_ge(o_stored[u], 16 * (T // 8))

        @block.tensor
        def _(pe):
            M = nc.tensor

            def transpose_x(t):
                pe.wait_ge(xn_done, t.n + 1)
                pe.wait_ge(in_tile[t.par], t.half * 32 + 32)
                wait_past(pe, qT_sb, t.n - 1)
                for c in range(KC):
                    M.transpose(ps_tr[:, c * P:(c + 1) * P], xn[:, t.par, c * P:(c + 1) * P], ident[:])
                M.transpose(ps_tr[:, D:D + P], ctx_sb[:, t.par, :], ident[:]).then_inc(xT_done, 1)

            def project_qk(t):
                pe.wait_ge(xT_sb, t.n + 1)
                wait_past(pe, rope_done, t.n)
                for c in range(KC):
                    M.matmul(ps_qk[:, 0:D], xT[:, t.par, c * P:(c + 1) * P], wq_p[:, c, :],
                             start=(c == 0), stop=(c == KC - 1))
                M.matmul(ps_qk[:, D:2 * D], xT[:, t.par, D:D + P], wk_p[:], start=True, stop=True).then_inc(qk_done, 1)

            def project_v(t):
                pe.wait_ge(xT_sb, t.n + 1)
                wait_past(pe, x1_done, t.n - 2)
                for b in range(2):
                    for o in range(2):
                        ins = M.matmul(ps_vo[64 * o:64 * o + 64, D + b * P:D + (b + 1) * P],
                                       xT[:, t.par, D + 64 * b:D + 64 * b + 64], wv_p[:, o, :], start=True, stop=True)
                ins.then_inc(v_done, 1)

            def transpose_kq(t):
                pe.wait_ge(rot_done, t.n + 1)
                pe.wait_ge(xT_sb, upto(t.n + 2))
                wait_past(pe, x2T_sb, t.n - 3)
                for first, into in ((D, 0), (0, D)):
                    for c in range(KC):
                        ins = M.transpose(ps_tr[:, into + c * P:into + (c + 1) * P],
                                          rot[:, first + c * P:first + (c + 1) * P], ident[:])
                ins.then_inc(kqT_done, 1)

            def logits(t, g):
                pe.wait_ge(km_done, t.times(G, g + 1))
                if g == 0:
                    pe.wait_ge(qT_sb, t.n + 1)
                wait_past(pe, shift_done, t.times(G, g - 1))
                M.matmul(ps_l[g % 2][:], qbd[:, t.par, g, :], km[:, t.par, g].rearrange("p h k -> p (h k)"),
                         start=True, stop=True).then_inc(l_done, 1)

            def transpose_p(t, g):
                pe.wait_ge(exp_done, t.times(G, g + 1))
                wait_past(pe, pt_sb, t.times(G, g - 1))
                for j in range(G):
                    ins = M.transpose(ps_pt[g % 2][:, j * P:(j + 1) * P], expd[:, g % 2, j * P:(j + 1) * P], ident[:])
                ins.then_inc(pt_done, 1)

            def attend(t, c):
                pe.wait_ge(pt_sb, t.times(G, 2 * c + 2))
                if c == 0:
                    pe.wait_ge(v_sb, t.n + 1)
                    wait_past(pe, norm_done, t.n)
                probs = pT.rearrange("p g (j k) -> p (g j) k", k=P)
                for b in range(2):
                    for q in range(2):
                        for j in range(4):
                            pair = 8 * c + 2 * j + q
                            M.matmul(ps_nd[32 * j:32 * j + 32, c * P + 64 * b:c * P + 64 * b + 64],
                                     vst[:, t.par, 16 * b + pair, :], probs[:, pair, 64 * b:64 * b + 64],
                                     start=(q == 0), stop=(q == 1))
                for q in range(2):
                    for j in range(4):
                        ins = M.matmul(ps_nd[32 * j:32 * j + 32, D + c * P:D + (c + 1) * P], ones_pair[:, q, :],
                                       probs[:, 8 * c + 2 * j + q, :], start=(q == 0), stop=(q == 1))
                ins.then_inc(pv_done, 1)

            def project_out(t):
                pe.wait_ge(norm_done, t.n + 1)
                pe.wait_ge(v_sb, upto(t.n + 3))
                wait_past(pe, rank_read, t.n - 1)
                for c in range(KC):
                    ins = M.matmul(ps_vo[:, 0:D], attnT[:, c * P:(c + 1) * P], wout_sb[:, c, :],
                                   start=(c == 0), stop=(c == KC - 1))
                ins.then_inc(out_done, 1)

            def transpose_x1(t):
                pe.wait_ge(x2n_done, t.times(2, 1))
                pe.wait_ge(qT_sb, upto(t.n + 4))
                pe.wait_ge(xT_sb, upto(t.n + 6))
                for c in range(KC):
                    ins = M.transpose(ps_tr[:, c * P:(c + 1) * P], xs[:, t.par, 0, c * P:(c + 1) * P], ident[:])
                ins.then_inc(x2T_done, 1)

            def score(t):
                pe.wait_ge(x2T_sb, t.n + 1)
                pe.wait_ge(x1_done, upto(t.n + 2))
                pe.wait_ge(v_sb, upto(t.n + 5))
                wait_past(pe, rank_read, t.n)
                for c in range(KC):
                    ins = M.matmul(ps_vo[:, 0:E], x2T[:, c * P:(c + 1) * P], wgT[:, c, :],
                                   start=(c == 0), stop=(c == KC - 1))
                ins.then_inc(gate_done, 1)

            def rank(t):
                pe.wait_ge(top_done, t.n + 1)
                wait_past(pe, chosen_done, t.n)
                M.matmul(ps_vo[:, E:2 * E], tri[:], chosen[:], start=True, stop=False)
                M.matmul(ps_vo[:, E:2 * E], ones_bf[:], seen[:], start=False, stop=True).then_inc(rank_done, 1)

            def weights(t, slot):
                transpose_weights(banks_of(t, slot))

            def transpose_weights(which):
                for n in which:
                    kind, e, c = weight_bank(n)
                    if n == 0:
                        pe.wait_ge(shift_done, T * G)
                        pe.wait_ge(pt_sb, T * G)
                        pe.wait_ge(wf1_in, 32)
                    if n == E * KC:
                        pe.wait_ge(wf3_in, 32)
                    if n == E * KC + E:
                        pe.wait_ge(wf2_in, 32)
                    if n >= 4:
                        pe.wait_ge(wt_sb, n - 3)
                    ps = wt_banks[n % 4]
                    if kind == 3:
                        for h in range(2):
                            for d in range(KC):
                                ins = M.transpose(ps[0:HA, h * D + d * P:h * D + (d + 1) * P],
                                                  w3_raw[:, d, e, h * HB:h * HB + HA], ident[:])
                    else:
                        M.transpose(ps[:, 0:P], w12a[:, e, c * P:(c + 1) * P], ident[:])
                        ins = M.transpose(ps[:, P:H], w12b[:, e, c * P:(c + 1) * P], ident[0:H - P, 0:H - P])
                    ins.then_inc(wt_done, 1)

            pe.wait_ge(pool_const, N_POOL_CONST)
            pe.wait_ge(w_in, 16 * N_W)
            for c in range(KC):
                ins = M.transpose(ps_nd[:, c * E:(c + 1) * E], wg_raw[:, c * P:(c + 1) * P], ident[0:E, 0:E])
            ins.then_inc(wg_done, 1)
            pe.wait_ge(wg_sb, 1)
            pe.wait_ge(dve_const, N_DVE_CONST)
            pe.wait_ge(wqk_ready, KC + 2)

            def body(do, t):
                do(logits, t, 2)
                do(transpose_p, t, 0)
                do(transpose_kq, t.plus(1))
                do(attend, t.plus(-1), 1)
                weights(t, 0)

                do(logits, t, 3)
                do(project_v, t.plus(1))
                do(transpose_p, t, 1)
                do(transpose_x, t.plus(3))
                weights(t, 1)

                do(logits, t.plus(1), 0)
                do(score, t.plus(-3))
                do(transpose_p, t, 2)
                do(attend, t, 0)
                do(transpose_x1, t.plus(-2))
                weights(t, 2)

                do(logits, t.plus(1), 1)
                do(transpose_p, t, 3)
                do(rank, t.plus(-3))
                do(project_qk, t.plus(3))
                do(project_out, t.plus(-1))
                weights(t, 3)

            pipeline(pe, body)
            pe.wait_ge(chosen_done, T)
            pe.wait_ge(x1_done, T)
            M.matmul(ps_vo[:, 0:E], ones_bf[:], seen[:], start=True, stop=True).then_inc(cnt_done, 1)
            def transpose_block(b):
                pe.wait_ge(blk_in[b.slot(RB)], b.round(RB) * 16 + 16)
                wait_past(pe, bT_sb, b.n)
                for c in range(KC):
                    ins = M.transpose(ps_tr[:, c * P:(c + 1) * P], xb[:, b.slot(RB), c * P:(c + 1) * P], ident[:])
                ins.then_inc(bT_done, 1)

            ahead = [pe.alloc_register(f"expert{n}") for n in range(RB + 2)]
            experts, first_known = [], [0]

            def load_experts(first):
                count = min(RB + 2, NBLK - first) if isinstance(first, int) else RB + 2
                pe.load(ahead[:count], exp_i[0:1, bass.ds(first, count)])
                first_known[0] = first if isinstance(first, int) else 0
                experts[:] = [pe.snap(r, min_val=0, max_val=E - 1) for r in ahead[:count]]

            def expert_of(b):
                return experts[b.c - first_known[0]]

            def hidden(b):
                e = expert_of(b)
                pe.wait_ge(bT_sb, b.n + 1)
                wait_past(pe, gated_done, b.n - 1)
                parts = [(x, w, c) for c in range(KC) for x, w in ((x_hi, w12_hi), (x_hi, w12_lo), (x_lo, w12_hi))]
                for n, (x, w, c) in enumerate(parts):
                    ins = M.matmul(ps_h[b.par][:, 0:2 * H], x[:, b.par, c * P:(c + 1) * P],
                                   w[:, bass.ds(e, 1), c, :].rearrange("p a h -> p (a h)"),
                                   start=(n == 0), stop=(n == len(parts) - 1))
                ins.then_inc(h_done, 1)

            def transpose_hidden(b):
                pe.wait_ge(gated_done, b.n + 1)
                wait_past(pe, hT_sb, b.n - 1)
                for c in range(2):
                    ins = M.transpose(ps_hT[b.par][0:HA, c * P:(c + 1) * P], gated[:, b.par, c * HB:c * HB + HA], ident[:])
                ins.then_inc(hT_done, 1)

            def result(b):
                e = expert_of(b)
                pe.wait_ge(hT_sb, b.n + 1)
                wait_past(pe, y_copied, b.n - 1)
                parts = [(h, w, c) for c in range(2) for h, w in ((h_hi, w3_hi), (h_hi, w3_lo), (h_lo, w3_hi))]
                for n, (h, w, c) in enumerate(parts):
                    ins = M.matmul(ps_y[b.par][:, 0:D], h[:, b.par, c, :],
                                   w[:, bass.ds(e, 1), c, :].rearrange("p a d -> p (a d)"),
                                   start=(n == 0), stop=(n == len(parts) - 1))
                ins.then_inc(y_done, 1)

            def first_experts():
                pe.wait_ge(wdiff_done, 1)
                load_experts(0)

            last_weights(transpose_weights, transpose_block, first_experts)
            pe.wait_ge(wt_sb, NWT)
            pe.wait_ge(w3_zero, 2)

            def ffn_body(do, b):
                do(hidden, b)
                do(transpose_hidden, b.plus(-1))
                do(transpose_block, b.plus(2))
                do(result, b.plus(-2))

            blocks(pe, ffn_body, 2, load_experts)
    return nc


_INS = ['x', 'ctx_1024', 'fside_BxSx2_0', 'L0_xattn_Wq', 'L0_xattn_Wkv', 'L0_xattn_Wout', 'L0_xattn_bout',
        'L0_ffn_Wg', 'L0_ffn_W1', 'L0_ffn_W2', 'L0_ffn_W3']


def kernel(**inputs):
    import numpy as _np
    import concourse.bacc as _bacc
    from concourse import mybir as _mybir
    from concourse.bass_utils import run_bass_kernel_spmd as _run

    nc = _bacc.Bacc("TRN2", target_bir_lowering=False, num_devices=1)
    arrays, args = {}, []
    for name in _INS:
        a = _np.ascontiguousarray(inputs[name])
        arrays[f"in_{name}_dram"] = a
        args.append(nc.dram_tensor(f"in_{name}_dram", a.shape, _mybir.dt.from_np(a.dtype), kind="ExternalInput").ap())
    args.append(nc.dram_tensor("out_0_dram", (64, 64, 256), _mybir.dt.float32, kind="ExternalOutput").ap())
    xattn_ffn_kernel(nc, *args)
    r = _run(nc, [arrays], core_ids=[0])
    return r.results[0]["out_0_dram"]
```
